# Optimizing a Trainium2 kernel written in Bass

```python
import numpy as np
import jax
import jax.numpy as jnp

def _softmax(x, axis=-1):
    return jax.nn.softmax(x, axis=axis)

def _gelu(x):
    return jax.nn.gelu(x, approximate=True)

def _silu(x):
    return jax.nn.silu(x)

def _sigmoid(x):
    return jax.nn.sigmoid(x)

def _layernorm(x, axis=-1, eps=1e-05):
    m = jnp.mean(x, axis=axis, keepdims=True)
    v = jnp.var(x, axis=axis, keepdims=True)
    return (x - m) / jnp.sqrt(v + eps)

def _scatter_add(tgt, idx, src, axis=0):
    return tgt.at[idx].add(src)

def _segment_sum(src, seg, n):
    return jax.ops.segment_sum(src, seg, n)
kernel_name = 'mk_xattn_seq_d2_seqx_r4_cc0821'

def setup_inputs(seed: int=0):
    np.random.seed(seed)
    _w = jnp.asarray

    def _rec_inputs():
        import jax
        import jax.numpy as jnp
        _rk = jax.random.key(seed)
        x = 7.22e-05 + 1 * jax.random.normal(jax.random.fold_in(_rk, 1), (2, 512, 512), jnp.float32)
        _lenS = 512 - jax.random.randint(jax.random.fold_in(_rk, 7), (2,), 0, max(1, 512 // 4) + 1, jnp.int32)
        _lenS2 = 1024 - jax.random.randint(jax.random.fold_in(_rk, 8), (2,), 0, max(1, 1024 // 4) + 1, jnp.int32)
        _ctx_2048P = jax.random.normal(jax.random.fold_in(_rk, 11), (2, 16, 512), jnp.float32)
        _ctx_2048c = jax.random.dirichlet(jax.random.fold_in(_rk, 511), 0.3 * jnp.ones((16,), jnp.float32), (2, 1024))
        _ctx_2048t = jnp.einsum('bsk,bkd->bsd', _ctx_2048c, _ctx_2048P)
        _ctx_2048t = _ctx_2048t * jax.lax.rsqrt(jnp.mean(jnp.square(_ctx_2048t)) + 1e-12) * 0.953939
        ctx_2048 = 0.000189249 + 0.0999589 * (_ctx_2048t + 0.3 * jax.random.normal(jax.random.fold_in(_rk, 611), (2, 1024, 512), jnp.float32))
        return (x, ctx_2048)
    x, ctx_2048 = _rec_inputs()

    def _L0_xattn_setup():
        import jax, jax.numpy as jnp
        import numpy as np
        E, H, L, B = (512, 32, 256, 4)
        S = E // H
        DM, DD = (32, 64)

        def _ln(x, w, b, eps=1e-05):
            m = x.mean(-1, keepdims=True)
            v = ((x - m) ** 2).mean(-1, keepdims=True)
            return (x - m) / jnp.sqrt(v + eps) * w + b

        def _block(x, state, ln1_w, ln1_b, ln2_w, ln2_b, maa_x, maa_w1, maa_w2, maa_stack, time_decay, td_w1, td_w2, u, Wr, Wk, Wv, Wg, Wo, gn_w, gn_b, ffn_maa_k, ffn_maa_r, Wfk, Wfr, Wfv):
            b, l, e = x.shape
            h = u.shape[0]
            s_ = e // h
            xa = _ln(x, ln1_w, ln1_b)
            sx = jnp.concatenate([state[:, 1:2] - xa[:, :1], xa[:, :-1] - xa[:, 1:]], axis=1)
            xxx = jnp.tanh((xa + sx * maa_x) @ maa_w1).reshape(b, l, 5, DM)
            xxx = jnp.einsum('blfd,fde->blfe', xxx, maa_w2)
            xm = xa[:, :, None] + sx[:, :, None] * (maa_stack + xxx)
            xk, xw, xv, xr, xg = (xm[:, :, j] for j in range(5))
            w = jnp.exp(-jnp.exp(time_decay + jnp.tanh(xw @ td_w1) @ td_w2)).reshape(b, l, h, s_)
            r = (xr @ Wr.T).reshape(b, l, h, s_)
            k = (xk @ Wk.T).reshape(b, l, h, s_)
            v = (xv @ Wv.T).reshape(b, l, h, s_)
            g = jax.nn.silu(xg @ Wg.T)
            s0 = state[:, 2:2 + s_].reshape(b, h, s_, s_)

            def step(s, rkvw):
                r_t, k_t, v_t, w_t = rkvw
                a = k_t[..., :, None] * v_t[..., None, :]
                out = jnp.einsum('bhi,bhij->bhj', r_t, u * a + s)
                s = a + w_t[..., :, None] * s
                return (s, out)
            rkvw = tuple((jnp.moveaxis(t, 1, 0) for t in (r, k, v, w)))
            _, out = jax.lax.scan(step, s0, rkvw)
            out = jnp.moveaxis(out, 0, 1).reshape(b, l, e)
            og = out.reshape(b, l, h, s_)
            m = og.mean(-1, keepdims=True)
            va = ((og - m) ** 2).mean(-1, keepdims=True)
            og = ((og - m) / jnp.sqrt(va + 1e-05)).reshape(b, l, e) * gn_w + gn_b
            x1 = x + og * g @ Wo.T
            xc = _ln(x1, ln2_w, ln2_b)
            sx2 = jnp.concatenate([state[:, 0:1] - xc[:, :1], xc[:, :-1] - xc[:, 1:]], axis=1)
            xk2 = xc + sx2 * ffn_maa_k
            xr2 = xc + sx2 * ffn_maa_r
            rr = jax.nn.sigmoid(xr2 @ Wfr.T)
            kk = jnp.square(jax.nn.relu(xk2 @ Wfk.T))
            return x1 + rr * (kk @ Wfv.T)
        key = jax.random.key(seed)
        ks = jax.random.split(key, 24)
        sc = 0.02
        d = {'x': jax.random.normal(ks[0], (B, L, E), jnp.float32), 'state': jax.random.normal(ks[1], (B, 2 + S, E), jnp.float32) * 0.1, 'ln1_w': jnp.ones((E,), jnp.float32), 'ln1_b': jnp.zeros((E,), jnp.float32), 'ln2_w': jnp.ones((E,), jnp.float32), 'ln2_b': jnp.zeros((E,), jnp.float32), 'maa_x': jax.random.normal(ks[2], (E,), jnp.float32) * 0.1, 'maa_w1': jax.random.normal(ks[3], (E, 5 * DM), jnp.float32) * sc, 'maa_w2': jax.random.normal(ks[4], (5, DM, E), jnp.float32) * sc, 'maa_stack': jax.random.normal(ks[5], (1, 5, E), jnp.float32) * 0.1, 'time_decay': jax.random.normal(ks[6], (E,), jnp.float32) * 0.5, 'td_w1': jax.random.normal(ks[7], (E, DD), jnp.float32) * sc, 'td_w2': jax.random.normal(ks[8], (DD, E), jnp.float32) * sc, 'u': jax.random.normal(ks[9], (H, S, 1), jnp.float32) * 0.1, 'Wr': jax.random.normal(ks[10], (E, E), jnp.float32) * sc, 'Wk': jax.random.normal(ks[11], (E, E), jnp.float32) * sc, 'Wv': jax.random.normal(ks[12], (E, E), jnp.float32) * sc, 'Wg': jax.random.normal(ks[13], (E, E), jnp.float32) * sc, 'Wo': jax.random.normal(ks[14], (E, E), jnp.float32) * sc, 'gn_w': jnp.ones((E,), jnp.float32), 'gn_b': jnp.zeros((E,), jnp.float32), 'ffn_maa_k': jax.random.normal(ks[15], (E,), jnp.float32) * 0.1, 'ffn_maa_r': jax.random.normal(ks[16], (E,), jnp.float32) * 0.1, 'Wfk': jax.random.normal(ks[17], (E, E), jnp.float32) * sc, 'Wfr': jax.random.normal(ks[18], (E, E), jnp.float32) * sc, 'Wfv': jax.random.normal(ks[19], (E, E), jnp.float32) * sc}
        return d
    _L0_xattn_all = _L0_xattn_setup()
    _L0_xattn_in = {k: v for k, v in _L0_xattn_all.items() if k in ('ln1_w', 'ln1_b', 'ln2_w', 'ln2_b', 'maa_x', 'maa_w1', 'maa_w2', 'maa_stack', 'time_decay', 'td_w1', 'td_w2', 'u', 'Wr', 'Wk', 'Wv', 'Wg', 'Wo', 'gn_w', 'gn_b', 'ffn_maa_k', 'ffn_maa_r', 'Wfk', 'Wfr', 'Wfv')}
    del _L0_xattn_all

    def _L1_xattn_setup():
        import jax, jax.numpy as jnp
        import numpy as np
        N_HEAD = 32
        EPS = 1e-05

        def _ln(x, w, b):
            m = jnp.mean(x, axis=-1, keepdims=True)
            v = jnp.mean((x - m) ** 2, axis=-1, keepdims=True)
            return (x - m) * jax.lax.rsqrt(v + EPS) * w + b

        def _forward(x, state, i, ln1_w, ln1_b, ln2_w, ln2_b, maa_x, maa_w, maa_k, maa_v, maa_r, maa_g, maa_w1, maa_w2, time_decay, decay_w1, decay_w2, faaaa, Wr, Wk, Wv, Wg, Wo, gn_w, gn_b, fmaa_k, fmaa_r, fWk, fWr, fWv):
            B, L, C = x.shape
            H = N_HEAD
            S = C // H
            i0 = (2 + S) * i
            xa = _ln(x, ln1_w, ln1_b)
            sx = jnp.concatenate([state[:, i0 + 1][:, None], xa[:, :-1]], axis=1) - xa
            xxx = xa + sx * maa_x
            t = jnp.tanh(xxx @ maa_w1).reshape(B, L, 5, -1)
            m = jnp.einsum('blfd,fdc->blfc', t, maa_w2)
            mw, mk, mv, mr, mg = (m[:, :, j] for j in range(5))
            xw = xa + sx * (maa_w + mw)
            xk = xa + sx * (maa_k + mk)
            xv = xa + sx * (maa_v + mv)
            xr = xa + sx * (maa_r + mr)
            xg = xa + sx * (maa_g + mg)
            w = time_decay + jnp.tanh(xw @ decay_w1) @ decay_w2
            w = jnp.exp(-jnp.exp(w)).reshape(B, L, H, S)
            r = (xr @ Wr.T).reshape(B, L, H, S)
            k = (xk @ Wk.T).reshape(B, L, H, S)
            v = (xv @ Wv.T).reshape(B, L, H, S)
            g = jax.nn.silu(xg @ Wg.T)
            s0 = state[:, i0 + 2:i0 + 2 + S].reshape(B, H, S, S)

            def step(s, inp):
                k_l, v_l, w_l, r_l = inp
                a = k_l[..., :, None] * v_l[..., None, :]
                out = jnp.einsum('bhs,bhst->bht', r_l, faaaa * a + s)
                s_new = a + w_l[..., None] * s
                return (s_new, out)
            seq = tuple((z.transpose(1, 0, 2, 3) for z in (k, v, w, r)))
            _, outs = jax.lax.scan(step, s0, seq)
            y = outs.transpose(1, 0, 2, 3)
            gm = jnp.mean(y, axis=-1, keepdims=True)
            gv = jnp.mean((y - gm) ** 2, axis=-1, keepdims=True)
            y = ((y - gm) * jax.lax.rsqrt(gv + EPS)).reshape(B, L, C) * gn_w + gn_b
            x = x + y * g @ Wo.T
            xc = _ln(x, ln2_w, ln2_b)
            sxc = jnp.concatenate([state[:, i0][:, None], xc[:, :-1]], axis=1) - xc
            xk2 = xc + sxc * fmaa_k
            xr2 = xc + sxc * fmaa_r
            rr = jax.nn.sigmoid(xr2 @ fWr.T)
            kk = jnp.square(jax.nn.relu(xk2 @ fWk.T))
            x = x + rr * (kk @ fWv.T)
            return x
        key = jax.random.key(seed)
        B, L, C, H = (8, 128, 512, N_HEAD)
        S = C // H
        DM, DD = (32, 64)
        ks = jax.random.split(key, 32)
        n = lambda k, shp, s=1.0: jax.random.normal(k, shp, dtype=jnp.float32) * s
        u = lambda k, shp: jax.random.uniform(k, shp, dtype=jnp.float32)
        inp = {'x': n(ks[0], (B, L, C)), 'state': n(ks[1], (B, 2 + S, C), 0.1), 'i': 0, 'ln1_w': jnp.ones((C,), jnp.float32), 'ln1_b': jnp.zeros((C,), jnp.float32), 'ln2_w': jnp.ones((C,), jnp.float32), 'ln2_b': jnp.zeros((C,), jnp.float32), 'maa_x': u(ks[2], (C,)), 'maa_w': u(ks[3], (C,)), 'maa_k': u(ks[4], (C,)), 'maa_v': u(ks[5], (C,)), 'maa_r': u(ks[6], (C,)), 'maa_g': u(ks[7], (C,)), 'maa_w1': n(ks[8], (C, 5 * DM), 0.02), 'maa_w2': n(ks[9], (5, DM, C), 0.02), 'time_decay': n(ks[10], (C,), 0.5), 'decay_w1': n(ks[11], (C, DD), 0.02), 'decay_w2': n(ks[12], (DD, C), 0.02), 'faaaa': n(ks[13], (H, S, 1), 0.1), 'Wr': n(ks[14], (C, C), 0.02), 'Wk': n(ks[15], (C, C), 0.02), 'Wv': n(ks[16], (C, C), 0.02), 'Wg': n(ks[17], (C, C), 0.02), 'Wo': n(ks[18], (C, C), 0.02), 'gn_w': jnp.ones((C,), jnp.float32), 'gn_b': jnp.zeros((C,), jnp.float32), 'fmaa_k': u(ks[19], (C,)), 'fmaa_r': u(ks[20], (C,)), 'fWk': n(ks[21], (C, C), 0.02), 'fWr': n(ks[22], (C, C), 0.02), 'fWv': n(ks[23], (C, C), 0.02)}
        return inp
    _L1_xattn_all = _L1_xattn_setup()
    _L1_xattn_in = {k: v for k, v in _L1_xattn_all.items() if k in ('ln1_w', 'ln1_b', 'ln2_w', 'ln2_b', 'maa_x', 'maa_w', 'maa_k', 'maa_v', 'maa_r', 'maa_g', 'maa_w1', 'maa_w2', 'time_decay', 'decay_w1', 'decay_w2', 'faaaa', 'Wr', 'Wk', 'Wv', 'Wg', 'Wo', 'gn_w', 'gn_b', 'fmaa_k', 'fmaa_r', 'fWk', 'fWr', 'fWv')}
    del _L1_xattn_all
    return {'x': x, 'ctx_2048': ctx_2048, 'L0_xattn_ln1_w': _L0_xattn_in['ln1_w'], 'L0_xattn_ln1_b': _L0_xattn_in['ln1_b'], 'L0_xattn_ln2_w': _L0_xattn_in['ln2_w'], 'L0_xattn_ln2_b': _L0_xattn_in['ln2_b'], 'L0_xattn_maa_x': _L0_xattn_in['maa_x'], 'L0_xattn_maa_w1': _L0_xattn_in['maa_w1'], 'L0_xattn_maa_w2': _L0_xattn_in['maa_w2'], 'L0_xattn_maa_stack': _L0_xattn_in['maa_stack'], 'L0_xattn_time_decay': _L0_xattn_in['time_decay'], 'L0_xattn_td_w1': _L0_xattn_in['td_w1'], 'L0_xattn_td_w2': _L0_xattn_in['td_w2'], 'L0_xattn_u': _L0_xattn_in['u'], 'L0_xattn_Wr': _L0_xattn_in['Wr'], 'L0_xattn_Wk': _L0_xattn_in['Wk'], 'L0_xattn_Wv': _L0_xattn_in['Wv'], 'L0_xattn_Wg': _L0_xattn_in['Wg'], 'L0_xattn_Wo': _L0_xattn_in['Wo'], 'L0_xattn_gn_w': _L0_xattn_in['gn_w'], 'L0_xattn_gn_b': _L0_xattn_in['gn_b'], 'L0_xattn_ffn_maa_k': _L0_xattn_in['ffn_maa_k'], 'L0_xattn_ffn_maa_r': _L0_xattn_in['ffn_maa_r'], 'L0_xattn_Wfk': _L0_xattn_in['Wfk'], 'L0_xattn_Wfr': _L0_xattn_in['Wfr'], 'L0_xattn_Wfv': _L0_xattn_in['Wfv'], 'L1_xattn_ln1_w': _L1_xattn_in['ln1_w'], 'L1_xattn_ln1_b': _L1_xattn_in['ln1_b'], 'L1_xattn_ln2_w': _L1_xattn_in['ln2_w'], 'L1_xattn_ln2_b': _L1_xattn_in['ln2_b'], 'L1_xattn_maa_x': _L1_xattn_in['maa_x'], 'L1_xattn_maa_w': _L1_xattn_in['maa_w'], 'L1_xattn_maa_k': _L1_xattn_in['maa_k'], 'L1_xattn_maa_v': _L1_xattn_in['maa_v'], 'L1_xattn_maa_r': _L1_xattn_in['maa_r'], 'L1_xattn_maa_g': _L1_xattn_in['maa_g'], 'L1_xattn_maa_w1': _L1_xattn_in['maa_w1'], 'L1_xattn_maa_w2': _L1_xattn_in['maa_w2'], 'L1_xattn_time_decay': _L1_xattn_in['time_decay'], 'L1_xattn_decay_w1': _L1_xattn_in['decay_w1'], 'L1_xattn_decay_w2': _L1_xattn_in['decay_w2'], 'L1_xattn_faaaa': _L1_xattn_in['faaaa'], 'L1_xattn_Wr': _L1_xattn_in['Wr'], 'L1_xattn_Wk': _L1_xattn_in['Wk'], 'L1_xattn_Wv': _L1_xattn_in['Wv'], 'L1_xattn_Wg': _L1_xattn_in['Wg'], 'L1_xattn_Wo': _L1_xattn_in['Wo'], 'L1_xattn_gn_w': _L1_xattn_in['gn_w'], 'L1_xattn_gn_b': _L1_xattn_in['gn_b'], 'L1_xattn_fmaa_k': _L1_xattn_in['fmaa_k'], 'L1_xattn_fmaa_r': _L1_xattn_in['fmaa_r'], 'L1_xattn_fWk': _L1_xattn_in['fWk'], 'L1_xattn_fWr': _L1_xattn_in['fWr'], 'L1_xattn_fWv': _L1_xattn_in['fWv']}

def reference(x, ctx_2048, L0_xattn_ln1_w, L0_xattn_ln1_b, L0_xattn_ln2_w, L0_xattn_ln2_b, L0_xattn_maa_x, L0_xattn_maa_w1, L0_xattn_maa_w2, L0_xattn_maa_stack, L0_xattn_time_decay, L0_xattn_td_w1, L0_xattn_td_w2, L0_xattn_u, L0_xattn_Wr, L0_xattn_Wk, L0_xattn_Wv, L0_xattn_Wg, L0_xattn_Wo, L0_xattn_gn_w, L0_xattn_gn_b, L0_xattn_ffn_maa_k, L0_xattn_ffn_maa_r, L0_xattn_Wfk, L0_xattn_Wfr, L0_xattn_Wfv, L1_xattn_ln1_w, L1_xattn_ln1_b, L1_xattn_ln2_w, L1_xattn_ln2_b, L1_xattn_maa_x, L1_xattn_maa_w, L1_xattn_maa_k, L1_xattn_maa_v, L1_xattn_maa_r, L1_xattn_maa_g, L1_xattn_maa_w1, L1_xattn_maa_w2, L1_xattn_time_decay, L1_xattn_decay_w1, L1_xattn_decay_w2, L1_xattn_faaaa, L1_xattn_Wr, L1_xattn_Wk, L1_xattn_Wv, L1_xattn_Wg, L1_xattn_Wo, L1_xattn_gn_w, L1_xattn_gn_b, L1_xattn_fmaa_k, L1_xattn_fmaa_r, L1_xattn_fWk, L1_xattn_fWr, L1_xattn_fWv):
    import jax
    import jax.numpy as jnp

    def _L0_xattn_ref(x, state, ln1_w, ln1_b, ln2_w, ln2_b, maa_x, maa_w1, maa_w2, maa_stack, time_decay, td_w1, td_w2, u, Wr, Wk, Wv, Wg, Wo, gn_w, gn_b, ffn_maa_k, ffn_maa_r, Wfk, Wfr, Wfv):
        import jax, jax.numpy as jnp
        import numpy as np
        E, H, L, B = (512, 32, 256, 4)
        S = E // H
        DM, DD = (32, 64)

        def _ln(x, w, b, eps=1e-05):
            m = x.mean(-1, keepdims=True)
            v = ((x - m) ** 2).mean(-1, keepdims=True)
            return (x - m) / jnp.sqrt(v + eps) * w + b

        def _block(x, state, ln1_w, ln1_b, ln2_w, ln2_b, maa_x, maa_w1, maa_w2, maa_stack, time_decay, td_w1, td_w2, u, Wr, Wk, Wv, Wg, Wo, gn_w, gn_b, ffn_maa_k, ffn_maa_r, Wfk, Wfr, Wfv):
            b, l, e = x.shape
            h = u.shape[0]
            s_ = e // h
            xa = _ln(x, ln1_w, ln1_b)
            sx = jnp.concatenate([state[:, 1:2] - xa[:, :1], xa[:, :-1] - xa[:, 1:]], axis=1)
            xxx = jnp.tanh((xa + sx * maa_x) @ maa_w1).reshape(b, l, 5, DM)
            xxx = jnp.einsum('blfd,fde->blfe', xxx, maa_w2)
            xm = xa[:, :, None] + sx[:, :, None] * (maa_stack + xxx)
            xk, xw, xv, xr, xg = (xm[:, :, j] for j in range(5))
            w = jnp.exp(-jnp.exp(time_decay + jnp.tanh(xw @ td_w1) @ td_w2)).reshape(b, l, h, s_)
            r = (xr @ Wr.T).reshape(b, l, h, s_)
            k = (xk @ Wk.T).reshape(b, l, h, s_)
            v = (xv @ Wv.T).reshape(b, l, h, s_)
            g = jax.nn.silu(xg @ Wg.T)
            s0 = state[:, 2:2 + s_].reshape(b, h, s_, s_)

            def step(s, rkvw):
                r_t, k_t, v_t, w_t = rkvw
                a = k_t[..., :, None] * v_t[..., None, :]
                out = jnp.einsum('bhi,bhij->bhj', r_t, u * a + s)
                s = a + w_t[..., :, None] * s
                return (s, out)
            rkvw = tuple((jnp.moveaxis(t, 1, 0) for t in (r, k, v, w)))
            _, out = jax.lax.scan(step, s0, rkvw)
            out = jnp.moveaxis(out, 0, 1).reshape(b, l, e)
            og = out.reshape(b, l, h, s_)
            m = og.mean(-1, keepdims=True)
            va = ((og - m) ** 2).mean(-1, keepdims=True)
            og = ((og - m) / jnp.sqrt(va + 1e-05)).reshape(b, l, e) * gn_w + gn_b
            x1 = x + og * g @ Wo.T
            xc = _ln(x1, ln2_w, ln2_b)
            sx2 = jnp.concatenate([state[:, 0:1] - xc[:, :1], xc[:, :-1] - xc[:, 1:]], axis=1)
            xk2 = xc + sx2 * ffn_maa_k
            xr2 = xc + sx2 * ffn_maa_r
            rr = jax.nn.sigmoid(xr2 @ Wfr.T)
            kk = jnp.square(jax.nn.relu(xk2 @ Wfk.T))
            return x1 + rr * (kk @ Wfv.T)
        return _block(x, state, ln1_w, ln1_b, ln2_w, ln2_b, maa_x, maa_w1, maa_w2, maa_stack, time_decay, td_w1, td_w2, u, Wr, Wk, Wv, Wg, Wo, gn_w, gn_b, ffn_maa_k, ffn_maa_r, Wfk, Wfr, Wfv)

    def _L1_xattn_ref(x, state, i, ln1_w, ln1_b, ln2_w, ln2_b, maa_x, maa_w, maa_k, maa_v, maa_r, maa_g, maa_w1, maa_w2, time_decay, decay_w1, decay_w2, faaaa, Wr, Wk, Wv, Wg, Wo, gn_w, gn_b, fmaa_k, fmaa_r, fWk, fWr, fWv):
        import jax, jax.numpy as jnp
        import numpy as np
        N_HEAD = 32
        EPS = 1e-05

        def _ln(x, w, b):
            m = jnp.mean(x, axis=-1, keepdims=True)
            v = jnp.mean((x - m) ** 2, axis=-1, keepdims=True)
            return (x - m) * jax.lax.rsqrt(v + EPS) * w + b

        def _forward(x, state, i, ln1_w, ln1_b, ln2_w, ln2_b, maa_x, maa_w, maa_k, maa_v, maa_r, maa_g, maa_w1, maa_w2, time_decay, decay_w1, decay_w2, faaaa, Wr, Wk, Wv, Wg, Wo, gn_w, gn_b, fmaa_k, fmaa_r, fWk, fWr, fWv):
            B, L, C = x.shape
            H = N_HEAD
            S = C // H
            i0 = (2 + S) * i
            xa = _ln(x, ln1_w, ln1_b)
            sx = jnp.concatenate([state[:, i0 + 1][:, None], xa[:, :-1]], axis=1) - xa
            xxx = xa + sx * maa_x
            t = jnp.tanh(xxx @ maa_w1).reshape(B, L, 5, -1)
            m = jnp.einsum('blfd,fdc->blfc', t, maa_w2)
            mw, mk, mv, mr, mg = (m[:, :, j] for j in range(5))
            xw = xa + sx * (maa_w + mw)
            xk = xa + sx * (maa_k + mk)
            xv = xa + sx * (maa_v + mv)
            xr = xa + sx * (maa_r + mr)
            xg = xa + sx * (maa_g + mg)
            w = time_decay + jnp.tanh(xw @ decay_w1) @ decay_w2
            w = jnp.exp(-jnp.exp(w)).reshape(B, L, H, S)
            r = (xr @ Wr.T).reshape(B, L, H, S)
            k = (xk @ Wk.T).reshape(B, L, H, S)
            v = (xv @ Wv.T).reshape(B, L, H, S)
            g = jax.nn.silu(xg @ Wg.T)
            s0 = state[:, i0 + 2:i0 + 2 + S].reshape(B, H, S, S)

            def step(s, inp):
                k_l, v_l, w_l, r_l = inp
                a = k_l[..., :, None] * v_l[..., None, :]
                out = jnp.einsum('bhs,bhst->bht', r_l, faaaa * a + s)
                s_new = a + w_l[..., None] * s
                return (s_new, out)
            seq = tuple((z.transpose(1, 0, 2, 3) for z in (k, v, w, r)))
            _, outs = jax.lax.scan(step, s0, seq)
            y = outs.transpose(1, 0, 2, 3)
            gm = jnp.mean(y, axis=-1, keepdims=True)
            gv = jnp.mean((y - gm) ** 2, axis=-1, keepdims=True)
            y = ((y - gm) * jax.lax.rsqrt(gv + EPS)).reshape(B, L, C) * gn_w + gn_b
            x = x + y * g @ Wo.T
            xc = _ln(x, ln2_w, ln2_b)
            sxc = jnp.concatenate([state[:, i0][:, None], xc[:, :-1]], axis=1) - xc
            xk2 = xc + sxc * fmaa_k
            xr2 = xc + sxc * fmaa_r
            rr = jax.nn.sigmoid(xr2 @ fWr.T)
            kk = jnp.square(jax.nn.relu(xk2 @ fWk.T))
            x = x + rr * (kk @ fWv.T)
            return x
        return _forward(x, state, i, ln1_w, ln1_b, ln2_w, ln2_b, maa_x, maa_w, maa_k, maa_v, maa_r, maa_g, maa_w1, maa_w2, time_decay, decay_w1, decay_w2, faaaa, Wr, Wk, Wv, Wg, Wo, gn_w, gn_b, fmaa_k, fmaa_r, fWk, fWr, fWv)
    x = _L0_xattn_ref(x, ctx_2048, L0_xattn_ln1_w, L0_xattn_ln1_b, L0_xattn_ln2_w, L0_xattn_ln2_b, L0_xattn_maa_x, L0_xattn_maa_w1, L0_xattn_maa_w2, L0_xattn_maa_stack, L0_xattn_time_decay, L0_xattn_td_w1, L0_xattn_td_w2, L0_xattn_u, L0_xattn_Wr, L0_xattn_Wk, L0_xattn_Wv, L0_xattn_Wg, L0_xattn_Wo, L0_xattn_gn_w, L0_xattn_gn_b, L0_xattn_ffn_maa_k, L0_xattn_ffn_maa_r, L0_xattn_Wfk, L0_xattn_Wfr, L0_xattn_Wfv)
    x = _L1_xattn_ref(x, ctx_2048, 0, L1_xattn_ln1_w, L1_xattn_ln1_b, L1_xattn_ln2_w, L1_xattn_ln2_b, L1_xattn_maa_x, L1_xattn_maa_w, L1_xattn_maa_k, L1_xattn_maa_v, L1_xattn_maa_r, L1_xattn_maa_g, L1_xattn_maa_w1, L1_xattn_maa_w2, L1_xattn_time_decay, L1_xattn_decay_w1, L1_xattn_decay_w2, L1_xattn_faaaa, L1_xattn_Wr, L1_xattn_Wk, L1_xattn_Wv, L1_xattn_Wg, L1_xattn_Wo, L1_xattn_gn_w, L1_xattn_gn_b, L1_xattn_fmaa_k, L1_xattn_fmaa_r, L1_xattn_fWk, L1_xattn_fWr, L1_xattn_fWv)
    return x

_drawn_inputs = setup_inputs


def setup_inputs(seed=0):
    import zlib

    import numpy as np

    out = dict(_drawn_inputs(seed))
    spreads = {'L0_xattn_ln1_w': (1.0, 0.2),
     'L0_xattn_ln1_b': (0.0, 0.1),
     'L0_xattn_ln2_w': (1.0, 0.6),
     'L0_xattn_ln2_b': (0.0, 0.8),
     'L0_xattn_gn_w': (1.0, 0.6),
     'L0_xattn_gn_b': (0.0, 0.652),
     'L1_xattn_ln1_w': (1.0, 0.2),
     'L1_xattn_ln1_b': (0.0, 0.288),
     'L1_xattn_ln2_w': (1.0, 0.6),
     'L1_xattn_ln2_b': (0.0, 0.8),
     'L1_xattn_gn_w': (1.0, 0.6),
     'L1_xattn_gn_b': (0.0, 0.8)}
    factors = {'ctx_2048': 26.553,
     'L0_xattn_maa_x': 8.0,
     'L0_xattn_maa_w1': 2.774,
     'L0_xattn_maa_w2': 2.826,
     'L0_xattn_td_w1': 8.0,
     'L0_xattn_td_w2': 8.0,
     'L0_xattn_u': 2.866,
     'L0_xattn_ffn_maa_k': 5.534,
     'L0_xattn_ffn_maa_r': 8.0,
     'L0_xattn_Wfr': 3.881,
     'L1_xattn_maa_x': 6.659,
     'L1_xattn_maa_w': 8.0,
     'L1_xattn_maa_w1': 3.488,
     'L1_xattn_maa_w2': 3.537,
     'L1_xattn_decay_w1': 8.0,
     'L1_xattn_decay_w2': 8.0,
     'L1_xattn_faaaa': 3.679,
     'L1_xattn_fmaa_r': 8.0,
     'L1_xattn_fWr': 7.655}
    for name, (base, spread) in spreads.items():
        noise = np.random.default_rng([zlib.crc32(name.encode()), seed]).standard_normal(out[name].shape)
        drawn = base * np.exp(spread * noise) if base else spread * noise
        out[name] = jnp.asarray(drawn.astype(out[name].dtype))
    for name, factor in factors.items():
        out[name] = (out[name] * factor).astype(out[name].dtype)
    return out
```

```python
import concourse.bass as bass
from concourse import mybir
from contextlib import ExitStack

P = 128
E = 512
G = E // P
B = 2
S = 512
NL = 2
HS = 16
T = 128
NT = S // T
C = G * B
BT = B * T
U = C * T
BANK = 512
DM, DD, NF = 32, 64, 5
LEVELS = 7
PAIR_LEVELS = 4
LN_EPS = 1e-5
(V_LN1W, V_LN1B, V_LN2W, V_LN2B, V_MAAX, V_MAA0, V_TD, V_U, V_GNW, V_GNB, V_FK, V_FR) = \
    (0, 1, 2, 3, 4, 5, 10, 11, 12, 13, 14, 15)
NV = 16
ORDER = [4, LEVELS, 5, 6]
VEC_LAYER, VEC_TILE = 13, 100


def build(nc, x_in, vec_in, maa1_in, maa2_in, dec1_in, dec2_in, sq_in, st_in, const_in, out):
    fp32 = mybir.dt.float32
    ALU = mybir.AluOpType
    ACT = mybir.ActivationFunctionType
    AX = mybir.AxisListType

    ctx = ExitStack()
    with ctx:
        def sb(name, shape):
            return ctx.enter_context(nc.sbuf_tensor(name, shape, fp32))

        def ps(name, cols):
            return ctx.enter_context(nc.psum_tensor(name, [P, cols], fp32))

        def sem(name):
            return ctx.enter_context(nc.semaphore(name))

        X = sb("X", [P, G, B, S])
        SQW = ("Wk", "Wv", "Wr", "Wg", "Wo", "Wfk", "Wfr", "Wfv")
        W = {k: sb(k, [P, G, E]) for k in SQW}
        MAA1 = sb("MAA1", [P, G, NF * DM])
        MAA2 = sb("MAA2", [P, E])
        MAA2B = sb("MAA2B", [DM, E])
        DEC1 = sb("DEC1", [P, G, DD])
        DEC2 = sb("DEC2", [DD, E])
        VEC = sb("VEC", [P, NV, G])
        CONST = sb("CONST", [P, 4 * P + 2])
        IDENT, HEAD, HEADMEAN, CHMEAN = (CONST[:, i * P:(i + 1) * P] for i in range(4))
        LMASK, EPS = CONST[:, 4 * P:4 * P + 1], CONST[:, 4 * P + 1:4 * P + 2]
        HEADU = sb("HEADU", [P, G, P])
        CTX0 = sb("CTX0", [P, C * HS + 2 * C])
        XA = sb("XA", [P, G, B, T + 1])
        CARRYA = sb("CARRYA", [P, G, B])
        CARRYC = sb("CARRYC", [P, G, B])
        SX = sb("SX", [P, G, B, T])
        XM = sb("XM", [P, G, B, T])
        SQ = sb("SQ", [P, G, B, T])
        RSTD = sb("RSTD", [P, B, T])
        TH1 = sb("TH1", [P, BT])
        TH2 = sb("TH2", [DM, BT])
        DTH = sb("DTH", [DD, BT])
        MX = [sb(f"MX{i}", [P, G, B, T]) for i in range(2)]
        RB = [sb(f"RB{i}", [P, U]) for i in range(4)]
        KB = [sb(f"KB{i}", [P, U]) for i in range(3)]
        WT = sb("WT", [P, 2 * U])
        VB = sb("VB", [P, U])
        GT = sb("GT", [P, U])
        OE = sb("OE", [P, U])
        NPR = 3
        PR = [sb(f"PR{i}", [P, BANK]) for i in range(NPR)]
        QB = sb("QB", [P, BANK])
        RD = sb("RD", [P, BANK])
        VT = sb("VT", [P, C, P])
        KT = sb("KT", [P, C, P])
        ST = [sb(f"ST{i}", [P, C // 2, P]) for i in range(2)]
        STATE = sb("STATE", [P, C, P])
        PA = [ps(f"PA{i}", 2 * BANK) for i in range(2)]
        PO = ps("PO", 2 * BANK)
        EX = [ps(f"EX{i}", BANK) for i in range(2)]

        WOFF = [2 * U - (2 * U >> i) for i in range(LEVELS + 1)]

        def wt(i):
            return WT[:, WOFF[i]:WOFF[i] + (U >> i)]

        def halves(ap, m):
            v = ap.rearrange("p (k h t) -> p k h t", h=2, t=m)
            return v[:, :, 0, :], v[:, :, 1, :]

        def pairs(ap):
            v = ap.rearrange("p (k h) -> p k h", h=2)
            return v[:, :, 0], v[:, :, 1]

        def flat(t):
            return t[:, :, :, :].rearrange("p g b t -> p (g b t)")

        CHUNKS = [(-1, 0, BANK), (-1, BANK, BANK)]
        for i in range(PAIR_LEVELS):
            m = 1 << i
            nb = BANK // (m * m)
            CHUNKS += [(i, k, nb) for k in range(0, U // (2 * m), nb)]
        NCH = len(CHUNKS)
        CH_END = {i: max(n for n, c in enumerate(CHUNKS) if c[0] == i) + 1 for i in range(-1, PAIR_LEVELS)}
        TURNS = []
        for i in ORDER:
            for q in range(1 if i == LEVELS else T // (2 << i)):
                TURNS += [(i, q, h) for h in range(2)]
        NTURN = len(TURNS)
        APPLIED = [sum(u[0] != LEVELS for u in TURNS[:t + 1]) for t in range(NTURN)]
        NAPPLY = APPLIED[-1]

        names = """x_loaded const_loaded vec_loaded low_loaded big_loaded out_stored
            vec_order act_order pool_order
            mean_ready centred squared var_ready std_ready
            xxx_ready hid_ready hid_tanh mix_ready mix_scaled mixed
            dhid_ready dhid_tanh k_ready v_ready r_ready g_ready dec_ready
            k_copied v_copied r_copied g_tanh g_done decay_done
            scaled halves_copied product_ready pairs_summed pairs_used
            vt_ready vt_copied kt_ready kt_copied kv_ready kv_masked carry_used applied state_done
            wkv_ready gmean_ready gcentred gsquared gvar_ready gstd gated
            wo_ready x1_ready fk_in fr_in fk_ready fk_relu fk_squared fr_ready fr_tanh fv_ready tiles_done
            layer_consts""".split()
        s = {k: sem(k) for k in names}
        block = ctx.enter_context(nc.Block())

        @block.sync
        def _(sp):
            sp.dma_start(CONST[:, :], const_in).then_inc(s["const_loaded"], 16)
            sp.dma_start(CTX0[:, :], st_in[:, :]).then_inc(s["const_loaded"], 16)
            sp.dma_start(X[:, :, :, :], x_in).then_inc(s["x_loaded"], 16)
            with sp.Fori(0, NL) as l:
                sp.wait_ge(s["tiles_done"], l * NT + 1)
                sp.dma_start(VEC[:, :, :], vec_in[bass.ds(l, 1), :, :, :].rearrange("l p v g -> p (l v) g")).then_inc(s["vec_loaded"], 16)
                sp.dma_start(MAA1[:, :, :], maa1_in[bass.ds(l, 1), :, :, :].rearrange("l p g n -> p (l g) n")).then_inc(s["low_loaded"], 16)
                sp.dma_start(MAA2[:, :], maa2_in[bass.ds(l, 1), 0:P, :].rearrange("l p n -> p (l n)")).then_inc(s["low_loaded"], 16)
                sp.dma_start(MAA2B[:, :], maa2_in[bass.ds(l, 1), P:P + DM, :].rearrange("l p n -> p (l n)")).then_inc(s["low_loaded"], 16)
                sp.dma_start(DEC1[:, :, :], dec1_in[bass.ds(l, 1), :, :, :].rearrange("l p g n -> p (l g) n")).then_inc(s["low_loaded"], 16)
                sp.dma_start(DEC2[:, :], dec2_in[bass.ds(l, 1), :, :].rearrange("l p n -> p (l n)")).then_inc(s["low_loaded"], 16)
                for j, k in enumerate(SQW):
                    sp.dma_start(W[k][:, :, :], sq_in[bass.ds(l, 1), j, :, :, :].rearrange("l p g n -> p (l g) n")).then_inc(s["big_loaded"], 16)
            sp.wait_ge(s["tiles_done"], NL * NT + 1)
            sp.dma_start(out, X[:, :, :, :]).then_inc(s["out_stored"], 16)
            sp.wait_ge(s["out_stored"], 16)

        @block.gpsimd
        def _(pool):
            with pool.Fori(0, NL * NT) as n:
                pool.wait_ge(s["k_copied"], n + 1)
                pool.wait_ge(s["r_copied"], n + 1)
                for c, (i, k0, nb) in enumerate(CHUNKS):
                    if i >= 0 and c == CH_END[i - 1]:
                        pool.wait_ge(s["scaled"], n * LEVELS + i)
                        pool.wait_ge(s["halves_copied"], n * 2 * LEVELS + 2 * i)
                    if c >= NPR:
                        pool.wait_ge(s["pairs_summed"], n * NCH + c - NPR + 1)
                    o = PR[c % NPR]
                    if i < 0:
                        nc.gpsimd.tensor_tensor(o[:, :], RB[0][:, k0:k0 + nb], KB[0][:, k0:k0 + nb], ALU.mult).then_inc(s["product_ready"], 1)
                    else:
                        m = 1 << i
                        r = halves(RB[i % 4][:, :], m)[1][:, k0:k0 + nb, :]
                        k = halves(KB[i % 3][:, :], m)[0][:, k0:k0 + nb, :]
                        shape = [P, nb, m, m]
                        nc.gpsimd.tensor_tensor(o[:, :].rearrange("p (k t s) -> p k t s", t=m, s=m),
                                                r.unsqueeze(3).broadcast_to(shape), k.unsqueeze(2).broadcast_to(shape),
                                                ALU.mult).then_inc(s["product_ready"], 1)

        @block.scalar
        def _(act):
            def norm_part(n, k):
                act.wait_ge(s["centred"], 2 * n + k + 1)
                nc.scalar.activation(flat(SQ), flat(XM), ACT.Square).then_inc(s["squared"], 1)
                act.wait_ge(s["var_ready"], 2 * n + k + 1)
                nc.scalar.activation(RSTD[:, :, :], EX[1][:, 0:BT].rearrange("p (b t) -> p b t", b=B), ACT.Sqrt, bias=EPS).then_inc(s["std_ready"], 1)

            def kt_evac(n, j):
                act.wait_ge(s["kt_ready"], n * len(ORDER) + j + 1)
                if j > 0:
                    act.wait_ge(s["kv_ready"], n * NTURN + [u[0] for u in TURNS].index(ORDER[j]))
                scale = LMASK if ORDER[j] == 4 else 1.0
                nc.scalar.activation(KT[:, :, :].rearrange("p c t -> p (c t)"), PA[j % 2][:, :], ACT.Copy, scale=scale).then_inc(s["kt_copied"], 1)

            act.wait_ge(s["const_loaded"], 32)
            with act.Fori(0, NL * NT) as n:
                norm_part(n, 0)
                act.wait_ge(s["hid_ready"], n + 1)
                nc.scalar.activation(TH1[:, :], EX[0][:, 0:BT], ACT.Tanh)
                nc.scalar.activation(TH2[:, :], EX[0][0:DM, BT:2 * BT], ACT.Tanh).then_inc(s["hid_tanh"], 1)
                act.wait_ge(s["dhid_ready"], n + 1)
                nc.scalar.activation(DTH[:, :], EX[1][0:DD, 0:BT], ACT.Tanh).then_inc(s["dhid_tanh"], 1)
                act.wait_ge(s["k_ready"], n + 1)
                nc.scalar.activation(KB[0][:, :], PA[0][:, :], ACT.Copy).then_inc(s["k_copied"], 1)
                act.wait_ge(s["dec_ready"], n + 1)
                for g in range(G):
                    nc.scalar.activation(WT[:, g * BT:(g + 1) * BT], PA[1][:, g * BT:(g + 1) * BT], ACT.Exp,
                                         bias=VEC[:, V_TD, g:g + 1]).then_inc(s["act_order"], 1)
                act.wait_ge(s["act_order"], (n + 1) * G)
                nc.scalar.activation(wt(0), wt(0), ACT.Exp, scale=-1.0).then_inc(s["decay_done"], 1)
                act.wait_ge(s["v_ready"], n + 1)
                nc.scalar.activation(VB[:, :], PA[0][:, :], ACT.Copy).then_inc(s["v_copied"], 1)
                act.wait_ge(s["r_ready"], n + 1)
                nc.scalar.activation(RB[0][:, :], PO[:, :], ACT.Copy).then_inc(s["r_copied"], 1)
                act.wait_ge(s["g_ready"], n + 1)
                nc.scalar.activation(flat(SQ), PA[0][:, :], ACT.Tanh, scale=0.5).then_inc(s["g_tanh"], 1)
                for i in range(LEVELS):
                    m = 1 << i
                    if i == 0:
                        act.wait_ge(s["r_copied"], n + 1)
                    else:
                        act.wait_ge(s["scaled"], n * LEVELS + i)
                        act.wait_ge(s["halves_copied"], n * 2 * LEVELS + 2 * i)
                    if 0 <= i - 2 < PAIR_LEVELS:
                        act.wait_ge(s["product_ready"], n * NCH + CH_END[i - 2])
                    if i == 6:
                        act.wait_ge(s["kt_ready"], n * 4 + 1)
                    nc.scalar.activation(halves(RB[(i + 1) % 4][:, :], m)[0], halves(RB[i % 4][:, :], m)[0], ACT.Copy).then_inc(s["halves_copied"], 1)
                    nc.scalar.activation(halves(KB[(i + 1) % 3][:, :], m)[1], halves(KB[i % 3][:, :], m)[1], ACT.Copy).then_inc(s["halves_copied"], 1)
                    if i == 0:
                        act.wait_ge(s["vt_ready"], n + 1)
                        nc.scalar.activation(VT[:, :, :].rearrange("p c t -> p (c t)"), PA[1][:, :], ACT.Copy).then_inc(s["vt_copied"], 1)
                    if i == 5:
                        kt_evac(n, 0)
                for j in range(1, 4):
                    kt_evac(n, j)
                act.wait_ge(s["gcentred"], n + 1)
                nc.scalar.activation(flat(SQ), flat(XM), ACT.Square).then_inc(s["gsquared"], 1)
                act.wait_ge(s["gvar_ready"], n + 1)
                nc.scalar.activation(flat(SQ), PA[1][:, :], ACT.Sqrt, bias=EPS).then_inc(s["gstd"], 1)
                norm_part(n, 1)
                act.wait_ge(s["fk_ready"], n + 1)
                nc.scalar.activation(flat(XM), PA[0][:, :], ACT.Relu).then_inc(s["fk_relu"], 1)
                act.wait_ge(s["fk_relu"], n + 1)
                nc.scalar.activation(flat(XM), flat(XM), ACT.Square).then_inc(s["fk_squared"], 1)
                act.wait_ge(s["fr_ready"], n + 1)
                nc.scalar.activation(flat(SQ), PA[1][:, :], ACT.Tanh, scale=0.5).then_inc(s["fr_tanh"], 1)

        @block.tensor
        def _(pe):
            def square(out_ps, w, rhs, done):
                for go in range(G):
                    for gi in range(G):
                        last = nc.tensor.matmul(out_ps[:, go * BT:(go + 1) * BT], w[:, gi, go * P:(go + 1) * P],
                                                rhs[:, gi * BT:(gi + 1) * BT], start=(gi == 0), stop=(gi == G - 1))
                last.then_inc(done, 1)

            def stats(out_ps, rhs, done):
                for g in range(G):
                    last = nc.tensor.matmul(out_ps[:, 0:BT], CHMEAN, rhs(g), start=(g == 0), stop=(g == G - 1))
                last.then_inc(done, 1)

            def norm_part(n, k, t0):
                stats(EX[0], lambda g: X[:, g, :, bass.ds(t0, T)], s["mean_ready"])
                pe.wait_ge(s["squared"], 2 * n + k + 1)
                stats(EX[1], lambda g: flat(SQ)[:, g * BT:(g + 1) * BT], s["var_ready"])

            def mix(n, f, out_ps):
                w2, th = (MAA2[DM * f:DM * f + DM, :], TH1[DM * f:DM * f + DM, :]) if f < 4 else (MAA2B[:, :], TH2[:, :])
                for g in range(G):
                    last = nc.tensor.matmul(out_ps[:, g * BT:(g + 1) * BT], w2[:, g * P:(g + 1) * P], th, start=True, stop=True)
                last.then_inc(s["mix_ready"], 1)

            def transposes(out_ps, src, done):
                for c in range(C):
                    last = nc.tensor.transpose(out_ps[:, c * P:(c + 1) * P], src[:, c * T:(c + 1) * T], IDENT)
                last.then_inc(done, 1)

            def kv(n, t):
                i, q, h = TURNS[t]
                m = 1 << i
                lo, wide = (0, P) if i == LEVELS else (2 * m * q, max(m, DM))
                if t >= 2:
                    pe.wait_ge(s["kv_masked"], n * NTURN + t - 1)
                for j in range(C // 2):
                    c = h * (C // 2) + j
                    last = nc.tensor.matmul(EX[t % 2][:, j * P:(j + 1) * P], KT[lo:lo + wide, c, :], VT[lo:lo + wide, c, :],
                                            start=True, stop=True)
                last.then_inc(s["kv_ready"], 1)

            def apply(n, t):
                i, q, h = TURNS[t]
                m = 1 << i
                pe.wait_ge(s["kv_masked"], n * NTURN + t + 1)
                for j in range(C // 2):
                    c = h * (C // 2) + j
                    a = c * T + 2 * m * q + m
                    last = nc.tensor.matmul(PO[:, a:a + m], ST[t % 2][:, j, :], RB[i % 4][:, a:a + m],
                                            start=False, stop=(t >= NTURN - 2), skip_group_check=True)
                last.then_inc(s["applied"], 1)

            pe.wait_ge(s["const_loaded"], 32)
            pe.wait_ge(s["x_loaded"], 16)
            with pe.Fori(0, NL) as l:
                with pe.Fori(0, NT) as tau:
                    n = l * NT + tau
                    t0 = tau * T
                    pe.wait_ge(s["low_loaded"], (l + 1) * 5 * 16)
                    pe.wait_ge(s["big_loaded"], (l + 1) * len(SQW) * 16)
                    pe.wait_ge(s["tiles_done"], n + 1)
                    norm_part(n, 0, t0)
                    pe.wait_ge(s["xxx_ready"], n + 1)
                    for g in range(G):
                        nc.tensor.matmul(EX[0][:, 0:BT], MAA1[:, g, 0:P], flat(MX[1])[:, g * BT:(g + 1) * BT], start=(g == 0), stop=(g == G - 1))
                    for g in range(G):
                        last = nc.tensor.matmul(EX[0][0:DM, BT:2 * BT], MAA1[:, g, P:P + DM], flat(MX[1])[:, g * BT:(g + 1) * BT],
                                                start=(g == 0), stop=(g == G - 1))
                    last.then_inc(s["hid_ready"], 1)
                    pe.wait_ge(s["hid_tanh"], n + 1)
                    mix(n, 0, PA[0])
                    mix(n, 1, PA[1])
                    pe.wait_ge(s["mixed"], n * NF + 1)
                    for g in range(G):
                        last = nc.tensor.matmul(EX[1][0:DD, 0:BT], DEC1[:, g, :], flat(MX[0])[:, g * BT:(g + 1) * BT], start=(g == 0), stop=(g == G - 1))
                    last.then_inc(s["dhid_ready"], 1)
                    mix(n, 2, PO)
                    pe.wait_ge(s["mixed"], n * NF + 2)
                    square(PA[0], W["Wk"], flat(MX[1]), s["k_ready"])
                    pe.wait_ge(s["dhid_tanh"], n + 1)
                    for g in range(G):
                        last = nc.tensor.matmul(PA[1][:, g * BT:(g + 1) * BT], DEC2[:, g * P:(g + 1) * P], DTH[:, :], start=True, stop=True)
                    last.then_inc(s["dec_ready"], 1)
                    pe.wait_ge(s["mixed"], n * NF + 3)
                    mix(n, 3, PO)
                    pe.wait_ge(s["k_copied"], n + 1)
                    square(PA[0], W["Wv"], flat(MX[0]), s["v_ready"])
                    pe.wait_ge(s["decay_done"], n + 1)
                    mix(n, 4, PA[1])
                    pe.wait_ge(s["mixed"], n * NF + 4)
                    square(PO, W["Wr"], flat(MX[1]), s["r_ready"])
                    pe.wait_ge(s["mixed"], n * NF + 5)
                    pe.wait_ge(s["v_copied"], n + 1)
                    square(PA[0], W["Wg"], flat(MX[0]), s["g_ready"])
                    transposes(PA[1], VB, s["vt_ready"])
                    for c, (i, k0, nb) in enumerate(CHUNKS):
                        pe.wait_ge(s["product_ready"], n * NCH + c + 1)
                        if c >= 2:
                            pe.wait_ge(s["pairs_used"], n * NCH + c - 1)
                        if i < 0:
                            for j in range(2):
                                last = nc.tensor.matmul(EX[c % 2][:, j * BT:(j + 1) * BT], HEADU[:, 2 * c + j, :],
                                                        PR[c % NPR][:, j * BT:(j + 1) * BT], start=True, stop=True)
                        else:
                            last = nc.tensor.matmul(EX[c % 2][:, :], HEAD, PR[c % NPR][:, :], start=True, stop=True)
                        last.then_inc(s["pairs_summed"], 1)
                    pe.wait_ge(s["g_done"], n + 1)
                    pe.wait_ge(s["scaled"], n * LEVELS + 4)
                    pe.wait_ge(s["halves_copied"], n * 2 * LEVELS + 8)
                    transposes(PA[0], KB[4 % 3], s["kt_ready"])
                    pe.wait_ge(s["scaled"], (n + 1) * LEVELS)
                    pe.wait_ge(s["halves_copied"], (n + 1) * 2 * LEVELS)
                    pe.wait_ge(s["state_done"], n + l + 1)
                    pe.wait_ge(s["r_copied"], n + 1)
                    for c in range(C):
                        last = nc.tensor.matmul(PO[:, c * T:(c + 1) * T], STATE[:, c, :], RB[LEVELS % 4][:, c * T:(c + 1) * T],
                                                start=(c % (C // 2) == 0), stop=False, skip_group_check=True)
                    last.then_inc(s["carry_used"], 1)
                    pe.wait_ge(s["vt_copied"], n + 1)
                    pe.wait_ge(s["pairs_used"], (n + 1) * NCH)
                    for t in range(NTURN):
                        i, q, h = TURNS[t]
                        if q == 0 and h == 0:
                            j = ORDER.index(i)
                            pe.wait_ge(s["kt_copied"], n * 4 + j + 1)
                        kv(n, t)
                        if q == (0 if i == LEVELS else T // (2 << i) - 1) and h == 1 and j < 3:
                            transposes(PA[(j + 1) % 2], KB[ORDER[j + 1] % 3], s["kt_ready"])
                        if t >= 1 and TURNS[t - 1][0] != LEVELS:
                            apply(n, t - 1)
                    apply(n, NTURN - 1)
                    pe.wait_ge(s["wkv_ready"], n + 1)
                    for h in range(2):
                        last = nc.tensor.matmul(PA[0][:, h * BANK:(h + 1) * BANK], HEADMEAN, flat(XM)[:, h * BANK:(h + 1) * BANK], start=True, stop=True)
                    last.then_inc(s["gmean_ready"], 1)
                    pe.wait_ge(s["gsquared"], n + 1)
                    for h in range(2):
                        last = nc.tensor.matmul(PA[1][:, h * BANK:(h + 1) * BANK], HEADMEAN, flat(SQ)[:, h * BANK:(h + 1) * BANK], start=True, stop=True)
                    last.then_inc(s["gvar_ready"], 1)
                    pe.wait_ge(s["gated"], n + 1)
                    square(PA[0], W["Wo"], flat(XM), s["wo_ready"])
                    pe.wait_ge(s["x1_ready"], n + 1)
                    norm_part(n, 1, t0)
                    pe.wait_ge(s["fk_in"], n + 1)
                    square(PA[0], W["Wfk"], flat(MX[0]), s["fk_ready"])
                    pe.wait_ge(s["fr_in"], n + 1)
                    square(PA[1], W["Wfr"], flat(MX[1]), s["fr_ready"])
                    pe.wait_ge(s["fk_squared"], n + 1)
                    square(PO, W["Wfv"], flat(XM), s["fv_ready"])

        @block.vector
        def _(dve):
            base, done = [0], [0]

            def step(ins):
                done[0] += 1
                ins.then_inc(s["vec_order"], 1)

            def settle():
                dve.wait_ge(s["vec_order"], base[0] + done[0])

            def chain(ins):
                step(ins)
                settle()

            def xt(t0):
                return X[:, :, :, bass.ds(t0, T)]

            def norm_part(n, k, t0, vw, vb, carry):
                dve.wait_ge(s["mean_ready"], 2 * n + k + 1)
                mean = EX[0][:, 0:BT].rearrange("p (b t) -> p b t", b=B).unsqueeze(1).broadcast_to([P, G, B, T])
                nc.vector.tensor_tensor(XM[:, :, :, :], xt(t0), mean, ALU.subtract).then_inc(s["centred"], 1)
                chain(nc.vector.tensor_copy(XA[:, :, :, 0], carry[:, :, :]))
                dve.wait_ge(s["centred"], 2 * n + k + 1)
                dve.wait_ge(s["squared"], 2 * n + k + 1)
                dve.wait_ge(s["std_ready"], 2 * n + k + 1)
                chain(nc.vector.reciprocal(RSTD[:, :, :], RSTD[:, :, :]))
                chain(nc.vector.tensor_tensor(XM[:, :, :, :], XM[:, :, :, :], RSTD[:, :, :].unsqueeze(1).broadcast_to([P, G, B, T]), ALU.mult))
                for g in range(G):
                    step(nc.vector.tensor_scalar(XA[:, g, :, 1:T + 1], XM[:, g, :, :], VEC[:, vw, g:g + 1], VEC[:, vb, g:g + 1], ALU.mult, ALU.add))
                settle()
                step(nc.vector.tensor_copy(carry[:, :, :], XA[:, :, :, T]))
                chain(nc.vector.tensor_tensor(SX[:, :, :, :], XA[:, :, :, 0:T], XA[:, :, :, 1:T + 1], ALU.subtract))

            def toward(dst, v, done_sem):
                for g in range(G):
                    last = nc.vector.scalar_tensor_tensor(out=dst[:, g, :, :], in0=SX[:, g, :, :], scalar=VEC[:, v, g:g + 1],
                                                          in1=XA[:, g, :, 1:T + 1], op0=ALU.mult, op1=ALU.add)
                    if g < G - 1:
                        step(last)
                last.then_inc(done_sem, 1)

            def scale_level(n, i):
                m = 1 << i
                wl, wr = pairs(wt(i))
                nk = U // (2 * m)
                if 0 <= i - 2 < PAIR_LEVELS:
                    dve.wait_ge(s["product_ready"], n * NCH + CH_END[i - 2])
                if i == 6:
                    dve.wait_ge(s["kt_ready"], n * 4 + 1)
                step(nc.vector.tensor_tensor(halves(RB[(i + 1) % 4][:, :], m)[1], halves(RB[i % 4][:, :], m)[1],
                                             wl.unsqueeze(2).broadcast_to([P, nk, m]), ALU.mult))
                step(nc.vector.tensor_tensor(halves(KB[(i + 1) % 3][:, :], m)[0], halves(KB[i % 3][:, :], m)[0],
                                             wr.unsqueeze(2).broadcast_to([P, nk, m]), ALU.mult))
                nc.vector.tensor_tensor(wt(i + 1), wl, wr, ALU.mult).then_inc(s["scaled"], 1)
                dve.wait_ge(s["scaled"], n * LEVELS + i + 1)
                dve.wait_ge(s["halves_copied"], n * 2 * LEVELS + 2 * (i + 1))

            def use_chunks(n, lo, hi):
                for c in range(lo, hi):
                    i, k0, nb = CHUNKS[c]
                    dve.wait_ge(s["pairs_summed"], n * NCH + c + 1)
                    if i < 0:
                        nc.vector.tensor_tensor(OE[:, k0:k0 + nb], EX[c % 2][:, :], VB[:, k0:k0 + nb], ALU.mult).then_inc(s["pairs_used"], 1)
                        dve.wait_ge(s["pairs_used"], n * NCH + c + 1)
                        continue
                    m = 1 << i
                    v = halves(VB[:, :], m)[0][:, k0:k0 + nb, :]
                    o = halves(OE[:, :], m)[1][:, k0:k0 + nb, :]
                    nc.vector.tensor_tensor(QB[:, :].rearrange("p (k t s) -> p k t s", t=m, s=m),
                                            EX[c % 2][:, :].rearrange("p (k t s) -> p k t s", t=m, s=m),
                                            v.unsqueeze(2).broadcast_to([P, nb, m, m]), ALU.mult).then_inc(s["pairs_used"], 1)
                    dve.wait_ge(s["pairs_used"], n * NCH + c + 1)
                    if m == 1:
                        part = QB[:, :].rearrange("p (k t) -> p k t", t=1)
                    else:
                        chain(nc.vector.tensor_reduce(out=RD[:, 0:nb * m].rearrange("p (k t) -> p k t", t=m),
                                                      in_=QB[:, :].rearrange("p (k t s) -> p k t s", t=m, s=m), axis=AX.X, op=ALU.add))
                        part = RD[:, 0:nb * m].rearrange("p (k t) -> p k t", t=m)
                    chain(nc.vector.tensor_tensor(o, o, part, ALU.add))

            dve.wait_ge(s["const_loaded"], 32)
            dve.wait_ge(s["x_loaded"], 16)
            nc.vector.memset(RD[:, 0:1], 0.0).then_inc(s["tiles_done"], 1)
            with nc.vector.Fori(0, NL) as l:
                dve.wait_ge(s["vec_loaded"], (l + 1) * 16)
                base[0], done[0] = l * (VEC_LAYER + NT * VEC_TILE), 0
                st = CTX0[:, 0:C * HS].rearrange("p (c j) -> p c j", c=C).unsqueeze(2).broadcast_to([P, C, P // HS, HS])
                hd = HEAD.rearrange("p (h j) -> p h j", j=HS)
                for c in range(C):
                    step(nc.vector.tensor_tensor(STATE[:, c, :].rearrange("p (h j) -> p h j", j=HS), st[:, c, :, :], hd, ALU.mult))
                step(nc.vector.tensor_copy(CARRYC[:, :, :], CTX0[:, C * HS:C * HS + C].rearrange("p (g b) -> p g b", g=G)))
                step(nc.vector.tensor_copy(CARRYA[:, :, :], CTX0[:, C * HS + C:C * HS + 2 * C].rearrange("p (g b) -> p g b", g=G)))
                for g in range(G):
                    last = nc.vector.tensor_scalar(HEADU[:, g, :], HEAD, VEC[:, V_U, g:g + 1], None, ALU.mult)
                    if g < G - 1:
                        step(last)
                last.then_inc(s["state_done"], 1)
                assert done[0] == VEC_LAYER, done
                with nc.vector.Fori(0, NT) as tau:
                    n = l * NT + tau
                    t0 = tau * T
                    base[0], done[0] = l * (VEC_LAYER + NT * VEC_TILE) + VEC_LAYER + tau * VEC_TILE, 0
                    dve.wait_ge(s["state_done"], n + l + 1)
                    norm_part(n, 0, t0, V_LN1W, V_LN1B, CARRYA)
                    toward(MX[1], V_MAAX, s["xxx_ready"])
                    for f in range(NF):
                        mx, pm = MX[f % 2], [PA[0], PA[1], PO, PO, PA[1]][f]
                        dve.wait_ge(s["mix_ready"], n * NF + f + 1)
                        dve.wait_ge(s[["hid_ready", "hid_ready", "dhid_ready", "k_ready", "v_ready"][f]], n + 1)
                        for g in range(G):
                            step(nc.vector.scalar_tensor_tensor(out=mx[:, g, :, :], in0=pm[:, g * BT:(g + 1) * BT].rearrange("p (b t) -> p b t", b=B),
                                                                scalar=VEC[:, V_MAA0 + f, g:g + 1], in1=SX[:, g, :, :], op0=ALU.add, op1=ALU.mult))
                        settle()
                        nc.vector.tensor_tensor(mx[:, :, :, :], mx[:, :, :, :], XA[:, :, :, 1:T + 1], ALU.add).then_inc(s["mixed"], 1)
                    dve.wait_ge(s["g_tanh"], n + 1)
                    nc.vector.scalar_tensor_tensor(out=GT[:, :], in0=flat(SQ), scalar=1.0, in1=PA[0][:, :], op0=ALU.add, op1=ALU.mult).then_inc(s["g_done"], 1)
                    dve.wait_ge(s["decay_done"], n + 1)
                    dve.wait_ge(s["k_copied"], n + 1)
                    dve.wait_ge(s["r_copied"], n + 1)
                    dve.wait_ge(s["v_copied"], n + 1)
                    scale_level(n, 0)
                    scale_level(n, 1)
                    use_chunks(n, 0, CH_END[0])
                    scale_level(n, 2)
                    use_chunks(n, CH_END[0], CH_END[1])
                    scale_level(n, 3)
                    use_chunks(n, CH_END[1], CH_END[2])
                    scale_level(n, 4)
                    use_chunks(n, CH_END[2], CH_END[3])
                    scale_level(n, 5)
                    scale_level(n, 6)
                    hmask = HEAD.unsqueeze(1).broadcast_to([P, C // 2, P])
                    for t, (i, q, h) in enumerate(TURNS):
                        dve.wait_ge(s["kv_ready"], n * NTURN + t + 1)
                        if t >= 2:
                            dve.wait_ge(s["applied"], n * NAPPLY + APPLIED[t - 2])
                        nc.vector.tensor_tensor(ST[t % 2][:, :, :], EX[t % 2][:, :].rearrange("p (c j) -> p c j", c=C // 2), hmask, ALU.mult).then_inc(s["kv_masked"], 1)
                        if i == LEVELS:
                            rows = STATE[:, h * (C // 2):(h + 1) * (C // 2), :]
                            dec = wt(LEVELS)[:, h * (C // 2):(h + 1) * (C // 2)].unsqueeze(2).broadcast_to([P, C // 2, P])
                            dve.wait_ge(s["carry_used"], n + 1)
                            chain(nc.vector.tensor_tensor(rows, rows, dec, ALU.mult))
                            dve.wait_ge(s["kv_masked"], n * NTURN + t + 1)
                            last = nc.vector.tensor_tensor(rows, rows, ST[t % 2][:, :, :], ALU.add)
                            if h == 0:
                                chain(last)
                            else:
                                last.then_inc(s["state_done"], 1)
                                dve.wait_ge(s["state_done"], n + l + 2)
                    dve.wait_ge(s["applied"], (n + 1) * NAPPLY)
                    nc.vector.tensor_tensor(flat(XM), PO[:, :], OE[:, :], ALU.add).then_inc(s["wkv_ready"], 1)
                    dve.wait_ge(s["gmean_ready"], n + 1)
                    nc.vector.tensor_tensor(flat(XM), flat(XM), PA[0][:, :], ALU.subtract).then_inc(s["gcentred"], 1)
                    dve.wait_ge(s["gstd"], n + 1)
                    dve.wait_ge(s["gcentred"], n + 1)
                    chain(nc.vector.reciprocal(flat(SQ), flat(SQ)))
                    chain(nc.vector.tensor_tensor(flat(XM), flat(XM), flat(SQ), ALU.mult))
                    for g in range(G):
                        step(nc.vector.tensor_scalar(XM[:, g, :, :], XM[:, g, :, :], VEC[:, V_GNW, g:g + 1], VEC[:, V_GNB, g:g + 1], ALU.mult, ALU.add))
                    settle()
                    nc.vector.scalar_tensor_tensor(out=flat(XM), in0=flat(XM), scalar=0.5, in1=GT[:, :], op0=ALU.mult, op1=ALU.mult).then_inc(s["gated"], 1)
                    dve.wait_ge(s["wo_ready"], n + 1)
                    nc.vector.tensor_tensor(xt(t0), xt(t0), PA[0][:, :].rearrange("p (g b t) -> p g b t", g=G, b=B), ALU.add).then_inc(s["x1_ready"], 1)
                    dve.wait_ge(s["x1_ready"], n + 1)
                    norm_part(n, 1, t0, V_LN2W, V_LN2B, CARRYC)
                    toward(MX[0], V_FK, s["fk_in"])
                    toward(MX[1], V_FR, s["fr_in"])
                    dve.wait_ge(s["fr_tanh"], n + 1)
                    dve.wait_ge(s["fv_ready"], n + 1)
                    chain(nc.vector.scalar_tensor_tensor(out=flat(SQ), in0=flat(SQ), scalar=1.0, in1=PO[:, :], op0=ALU.add, op1=ALU.mult))
                    nc.vector.scalar_tensor_tensor(out=xt(t0).rearrange("p g b t -> p (g b) t"), in0=flat(SQ).rearrange("p (c t) -> p c t", c=C), scalar=0.5,
                                                   in1=xt(t0).rearrange("p g b t -> p (g b) t"), op0=ALU.mult, op1=ALU.add).then_inc(s["tiles_done"], 1)
                    dve.wait_ge(s["tiles_done"], n + 2)
                    assert done[0] == VEC_TILE, done




_VECS = [("ln1_w",) * 2, ("ln1_b",) * 2, ("ln2_w",) * 2, ("ln2_b",) * 2, ("maa_x",) * 2,
         (1, "maa_w"), (0, "maa_k"), (2, "maa_v"), (3, "maa_r"), (4, "maa_g"),
         ("time_decay",) * 2, ("u", "faaaa"), ("gn_w",) * 2, ("gn_b",) * 2, ("ffn_maa_k", "fmaa_k"), ("ffn_maa_r", "fmaa_r")]
_SQUARES = [("Wk", "Wk"), ("Wv", "Wv"), ("Wr", "Wr"), ("Wg", "Wg"), ("Wo", "Wo"), ("Wfk", "fWk"), ("Wfr", "fWr"), ("Wfv", "fWv")]


def kernel(**inputs):
    import numpy as np
    import concourse.bacc as bacc
    from concourse.bass_utils import run_bass_kernel_spmd

    a = {k: np.asarray(v) for k, v in inputs.items()}

    def chan(v):
        v = np.moveaxis(v, -1, 0)
        return np.ascontiguousarray(np.moveaxis(v.reshape(G, P, *v.shape[1:]), 0, 1))

    x = chan(a["x"])
    vecs = []
    for l, pre in enumerate(("L0_xattn_", "L1_xattn_")):
        cols = []
        for pair in _VECS:
            if isinstance(pair[0], int):
                cols.append(a["L0_xattn_maa_stack"][0, pair[0]] if l == 0 else a[pre + pair[1]])
            else:
                cols.append(a[pre + pair[l]].reshape(E))
        vecs.append(np.stack([chan(c) for c in cols], axis=1))
    order0 = [1, 0, 2, 3, 4]
    w1 = [a["L0_xattn_maa_w1"].reshape(E, NF, DM)[:, order0].reshape(E, NF * DM), a["L1_xattn_maa_w1"]]
    w2 = [a["L0_xattn_maa_w2"][order0].reshape(NF * DM, E), a["L1_xattn_maa_w2"].reshape(NF * DM, E)]
    maa1 = np.stack([w.reshape(G, P, NF * DM).transpose(1, 0, 2) for w in w1])
    maa2 = np.stack(w2)
    dec1 = np.stack([a[k].reshape(G, P, DD).transpose(1, 0, 2) for k in ("L0_xattn_td_w1", "L1_xattn_decay_w1")])
    dec2 = np.stack([a[k] for k in ("L0_xattn_td_w2", "L1_xattn_decay_w2")])
    squares = np.stack([np.stack([a[pre + pair[l]].T.reshape(G, P, E).transpose(1, 0, 2) for pair in _SQUARES])
                        for l, pre in enumerate(("L0_xattn_", "L1_xattn_"))])
    ctx_rows = a["ctx_2048"][:, 0:2 + HS]
    wkv = ctx_rows[:, 2:].reshape(B, G, P, HS).transpose(2, 1, 0, 3).reshape(P, C * HS)
    shift = [chan(ctx_rows[:, r]).reshape(P, C) for r in (0, 1)]
    st = np.concatenate([wkv] + shift, axis=1)
    head = np.kron(np.eye(P // HS, dtype=np.float32), np.ones((HS, HS), np.float32))
    row = np.arange(P)
    const = np.concatenate([np.eye(P, dtype=np.float32), head, head / np.float32(HS), np.full((P, P), 1.0 / E, np.float32),
                            (row % 32 < 16).astype(np.float32)[:, None], np.full((P, 1), LN_EPS, np.float32)], axis=1)
    arrays = {"x": x, "vec": np.stack(vecs), "maa1": maa1, "maa2": maa2, "dec1": dec1, "dec2": dec2,
              "squares": squares, "st": st, "const": const}
    arrays = {k: np.ascontiguousarray(v) for k, v in arrays.items()}
    nc = bacc.Bacc("TRN2", target_bir_lowering=False, num_devices=1)
    args = [nc.dram_tensor(k, v.shape, mybir.dt.from_np(v.dtype), kind="ExternalInput").ap() for k, v in arrays.items()]
    args.append(nc.dram_tensor("y", x.shape, mybir.dt.float32, kind="ExternalOutput").ap())
    build(nc, *args)
    r = run_bass_kernel_spmd(nc, [arrays], core_ids=[0])
    y = r.results[0]["y"]
    return np.ascontiguousarray(y.transpose(2, 3, 1, 0).reshape(B, S, E))
```

```python
import concourse.bass as bass
from concourse import mybir
from contextlib import ExitStack

P = 128
E = 512
G = E // P
B = 2
S = 512
NL = 2
HS = 16
T = 128
NT = S // T
C = G * B
BT = B * T
U = C * T
BANK = 512
DM, DD, NF = 32, 64, 5
LEVELS = 7
PAIR_LEVELS = 4
LN_EPS = 1e-5
(V_LN1W, V_LN1B, V_LN2W, V_LN2B, V_MAAX, V_MAA0, V_TD, V_U, V_GNW, V_GNB, V_FK, V_FR) = \
    (0, 1, 2, 3, 4, 5, 10, 11, 12, 13, 14, 15)
NV = 16
F_W, F_K, F_V, F_R, F_G = range(NF)
MXBUF = {F_W: 3, F_K: 0, F_V: 1, F_R: 2, F_G: 3}
ORDER = [PAIR_LEVELS, LEVELS, 5, 6]
VEC_FIRST, VEC_LAYER, VEC_TILE = 21, 12, 71


def build(nc, x_in, vec_in, maa1_in, maa2_in, dec1_in, dec2_in, sq_in, st_in, const_in, out):
    fp32 = mybir.dt.float32
    ALU = mybir.AluOpType
    ACT = mybir.ActivationFunctionType
    AX = mybir.AxisListType

    ctx = ExitStack()
    with ctx:
        def sb(name, shape):
            return ctx.enter_context(nc.sbuf_tensor(name, shape, fp32))

        def ps(name, cols):
            return ctx.enter_context(nc.psum_tensor(name, [P, cols], fp32))

        def sem(name):
            return ctx.enter_context(nc.semaphore(name))

        X = sb("X", [P, G, B, S])
        SQW = ("Wk", "Wv", "Wr", "Wg", "Wo", "Wfk", "Wfr", "Wfv")
        W = {k: sb(k, [P, G, E]) for k in SQW}
        MAA1 = sb("MAA1", [P, G, NF * DM])
        MAA2 = sb("MAA2", [P, E])
        LOWB = sb("LOWB", [P, E])
        MAA2B, DEC2 = LOWB[0:DM, :], LOWB[DD:2 * DD, :]
        DEC1 = sb("DEC1", [P, G, DD])
        VEC = sb("VEC", [P, NL, NV, G])
        CONST = sb("CONST", [P, 3 * P + 3])
        IDENT, HEAD, CHMEAN = (CONST[:, i * P:(i + 1) * P] for i in range(3))
        LMASK, EPS, ZERO = (CONST[:, 3 * P + i:3 * P + i + 1] for i in range(3))
        HEADU = sb("HEADU", [P, G, P])
        CTX0 = sb("CTX0", [P, C * HS + 2 * C])
        XA = sb("XA", [P, G, B, T + 1])
        CARRYA = sb("CARRYA", [P, G, B])
        CARRYC = sb("CARRYC", [P, G, B])
        SX = sb("SX", [P, G, B, T])
        XM = sb("XM", [P, G, B, T])
        SQ = sb("SQ", [P, G, B, T])
        RSTD = sb("RSTD", [P, B, T])
        TH1 = sb("TH1", [P, BT])
        THB = sb("THB", [P, BT])
        TH2, DTH = THB[0:DM, :], THB[DD:2 * DD, :]
        MX = [sb(f"MX{i}", [P, G, B, T]) for i in range(4)]
        RB = [sb(f"RB{i}", [P, U]) for i in range(4)]
        KB = [sb(f"KB{i}", [P, U]) for i in range(3)]
        WT = sb("WT", [P, 2 * U])
        VB = sb("VB", [P, U])
        GT = sb("GT", [P, U])
        OE = sb("OE", [P, U])
        NPR = 3
        PR = [sb(f"PR{i}", [P, BANK]) for i in range(NPR)]
        QB = sb("QB", [P, BANK])
        RD = sb("RD", [P, BANK])
        GMEAN = sb("GMEAN", [P, P // HS * C])
        GSTD = sb("GSTD", [P, P // HS * C])
        VT = sb("VT", [P, C, P])
        KT = sb("KT", [P, C, P])
        NST = 3
        ST = [sb(f"ST{i}", [P, C // 2, P]) for i in range(NST)]
        STATE = sb("STATE", [P, C, P])
        PT = ps("PT", 2 * BANK)
        PM = ps("PM", 2 * BANK)
        PO = ps("PO", 2 * BANK)
        EX = [ps(f"EX{i}", BANK) for i in range(2)]

        WOFF = [2 * U - (2 * U >> i) for i in range(LEVELS + 1)]

        def wt(i):
            return WT[:, WOFF[i]:WOFF[i] + (U >> i)]

        def halves(ap, m):
            v = ap.rearrange("p (k h t) -> p k h t", h=2, t=m)
            return v[:, :, 0, :], v[:, :, 1, :]

        def pairs(ap):
            v = ap.rearrange("p (k h) -> p k h", h=2)
            return v[:, :, 0], v[:, :, 1]

        def flat(t):
            return t[:, :, :, :].rearrange("p g b t -> p (g b t)")

        CHUNKS = [(-1, 0, BANK), (-1, BANK, BANK)]
        for i in range(PAIR_LEVELS):
            m = 1 << i
            nb = BANK // (m * m)
            CHUNKS += [(i, k, nb) for k in range(0, U // (2 * m), nb)]
        NCH = len(CHUNKS)
        CH_END = {i: max(n for n, c in enumerate(CHUNKS) if c[0] == i) + 1 for i in range(-1, PAIR_LEVELS)}
        TURNS = []
        for i in ORDER:
            for q in range(1 if i == LEVELS else T // (2 << i)):
                TURNS += [(i, q, h) for h in range(2)]
        NTURN = len(TURNS)
        APPLIED = [sum(u[0] != LEVELS for u in TURNS[:t + 1]) for t in range(NTURN)]
        NAPPLY = APPLIED[-1]
        FIRST_TURN = [[u[0] for u in TURNS].index(i) for i in ORDER]
        MIX_AFTER_PRODUCT = [14, 15, 16, 17, 17]
        MIX_AFTER_SUM = [11, 12, 14, 15, 16]
        MIX_AFTER_USE = [10, 12, 13, 14, 15]

        def half_rows(t, h):
            return t[:, h * (C // 2):(h + 1) * (C // 2), :].rearrange("p c t -> p (c t)")

        names = """const_loaded x_first x_rest vec_loaded low_loaded out_stored
            vec_order act_order
            mean_a centred_a squared_a var_a std_a
            mean_c centred_c squared_c var_c std_c
            xxx_ready hid_ready hid_tanh mix_ready mix_scaled mixed
            dhid_ready dhid_tanh k_ready v_ready r_ready g_ready dec_ready
            k_copied v_copied r_copied g_tanh g_done decay_done
            scaled halves_copied product_ready pairs_summed pairs_used
            vt_ready vt_copied kt_ready kt_copied kv_ready kv_masked carry_used applied state_done
            wkv_summed gcentred gsquared gvar_ready gstd gnormed gback gweighted gated
            normed_a weighted_a left_cleared
            wo_ready x1_ready fk_in fr_in fk_ready fk_relu fk_squared fr_ready fr_tanh fv_ready tiles_done""".split()
        s = {k: sem(k) for k in names}
        w_loaded = {k: sem("loaded_" + k) for k in SQW}
        block = ctx.enter_context(nc.Block())


        def tiles(eng, start_layer, tile):
            for l in range(NL):
                start_layer(l)
                with eng.Fori(0, NT - 1) as tau:
                    tile(l * NT + tau, l, tau, l, (tau + 1) * T)
                tile(l * NT + NT - 1, l, NT - 1, l + 1 if l + 1 < NL else None, 0)

        @block.sync
        def _(sp):
            def low(l):
                sp.dma_start(MAA1[:, :, :], maa1_in[l]).then_inc(s["low_loaded"], 16)
                sp.dma_start(MAA2[:, :], maa2_in[l, 0:P, :]).then_inc(s["low_loaded"], 16)
                sp.dma_start(MAA2B, maa2_in[l, P:P + DM, :]).then_inc(s["low_loaded"], 16)
                sp.dma_start(DEC1[:, :, :], dec1_in[l]).then_inc(s["low_loaded"], 16)
                sp.dma_start(DEC2, dec2_in[l]).then_inc(s["low_loaded"], 16)

            sp.dma_start(X[:, :, :, 0:T], x_in[:, :, :, 0:T]).then_inc(s["x_first"], 16)
            sp.dma_start(CONST[:, :], const_in).then_inc(s["const_loaded"], 16)
            sp.dma_start(CTX0[:, :], st_in[:, :]).then_inc(s["const_loaded"], 16)
            sp.dma_start(VEC[:, :, :, :], vec_in).then_inc(s["vec_loaded"], 16)
            low(0)
            for j, k in enumerate(SQW):
                sp.dma_start(W[k][:, :, :], sq_in[0, j]).then_inc(w_loaded[k], 16)
                if k == "Wg":
                    sp.dma_start(X[:, :, :, T:S], x_in[:, :, :, T:S]).then_inc(s["x_rest"], 16)
            for l in range(1, NL):
                sp.wait_ge(s["mix_ready"], l * NT * 2 * NF)
                sp.wait_ge(s["dhid_ready"], l * NT)
                sp.wait_ge(s["dec_ready"], l * NT)
                low(l)
                for j, k in enumerate(SQW):
                    sp.wait_ge(s[dict(Wk="k_ready", Wv="v_ready", Wr="r_ready", Wg="g_ready", Wo="wo_ready",
                                      Wfk="fk_ready", Wfr="fr_ready", Wfv="fv_ready")[k]], l * NT)
                    sp.dma_start(W[k][:, :, :], sq_in[l, j]).then_inc(w_loaded[k], 16)
            for tau in range(NT):
                sp.wait_ge(s["tiles_done"], (NL - 1) * NT + tau + 2)
                sp.dma_start(out[:, :, :, tau * T:(tau + 1) * T], X[:, :, :, tau * T:(tau + 1) * T]).then_inc(s["out_stored"], 16)
            sp.wait_ge(s["out_stored"], 16 * NT)

        @block.gpsimd
        def _(pool):
            def add_mix(m, f):
                pool.wait_ge(s["mix_scaled"], m * 2 * NF + 2 * f + 2)
                mx = MX[MXBUF[f]]
                nc.gpsimd.tensor_tensor(mx[:, :, :, :], mx[:, :, :, :], XA[:, :, :, 1:T + 1], ALU.add).then_inc(s["mixed"], 1)

            def products(n, lo, hi):
                for c in range(lo, hi):
                    i, k0, nb = CHUNKS[c]
                    if i >= 1 and c == CH_END[i - 1]:
                        pool.wait_ge(s["scaled"], n * LEVELS + i)
                        pool.wait_ge(s["halves_copied"], n * 2 * LEVELS + 2 * i)
                    if c >= NPR:
                        pool.wait_ge(s["pairs_summed"], n * NCH + c - NPR + 1)
                    o = PR[c % NPR]
                    if i < 0:
                        nc.gpsimd.tensor_tensor(o[:, :], RB[0][:, k0:k0 + nb], KB[0][:, k0:k0 + nb], ALU.mult).then_inc(s["product_ready"], 1)
                    else:
                        h = 1 << i
                        r = halves(RB[i % 4][:, :], h)[1][:, k0:k0 + nb, :]
                        k = halves(KB[i % 3][:, :], h)[0][:, k0:k0 + nb, :]
                        shape = [P, nb, h, h]
                        nc.gpsimd.tensor_tensor(o[:, :].rearrange("p (k t s) -> p k t s", t=h, s=h),
                                                r.unsqueeze(3).broadcast_to(shape), k.unsqueeze(2).broadcast_to(shape),
                                                ALU.mult).then_inc(s["product_ready"], 1)

            def tile(n, l, tau, ln, t0n):
                m = n + 1
                pool.wait_ge(s["k_copied"], n + 1)
                pool.wait_ge(s["r_copied"], n + 1)
                at = 0
                for f, upto in enumerate(MIX_AFTER_PRODUCT):
                    products(n, at, upto)
                    at = upto
                    if ln is not None:
                        add_mix(m, f)
                products(n, at, NCH)

            for f in range(NF):
                add_mix(0, f)
            tiles(pool, lambda l: None, tile)

        @block.scalar
        def _(act):
            def square_centred(m, k):
                act.wait_ge(s["centred_" + k], m + 1)
                nc.scalar.activation(flat(SQ), flat(XM), ACT.Square).then_inc(s["squared_" + k], 1)

            def deviation(m, k, var):
                act.wait_ge(s["var_" + k], m + 1)
                nc.scalar.activation(RSTD[:, :, :], var.rearrange("p (b t) -> p b t", b=B), ACT.Sqrt, bias=EPS).then_inc(s["std_" + k], 1)

            def weight_a(m, l):
                act.wait_ge(s["normed_a"], m + 1)
                for g in range(G):
                    last = nc.scalar.activation(XA[:, g, :, 1:T + 1], XM[:, g, :, :], ACT.Identity,
                                                scale=VEC[:, l, V_LN1W, g:g + 1], bias=VEC[:, l, V_LN1B, g:g + 1])
                last.then_inc(s["weighted_a"], 1)

            def hidden_tanh(m):
                act.wait_ge(s["hid_ready"], m + 1)
                nc.scalar.activation(TH1[:, :], PM[:, 0:BT], ACT.Tanh)
                nc.scalar.activation(TH2, PM[0:DM, BT:2 * BT], ACT.Tanh).then_inc(s["hid_tanh"], 1)

            def decay_hidden_tanh(m):
                act.wait_ge(s["dhid_ready"], m + 1)
                nc.scalar.activation(DTH, PM[DD:2 * DD, 0:BT], ACT.Tanh).then_inc(s["dhid_tanh"], 1)

            def take_k(m):
                act.wait_ge(s["k_ready"], m + 1)
                nc.scalar.activation(KB[0][:, :], PT[:, :], ACT.Copy).then_inc(s["k_copied"], 1)

            def take_decay(m, l):
                act.wait_ge(s["dec_ready"], m + 1)
                for g in range(G):
                    nc.scalar.activation(WT[:, g * BT:(g + 1) * BT], PM[:, g * BT:(g + 1) * BT], ACT.Exp,
                                         bias=VEC[:, l, V_TD, g:g + 1]).then_inc(s["act_order"], 1)
                act.wait_ge(s["act_order"], (m + 1) * G)
                nc.scalar.activation(wt(0), wt(0), ACT.Exp, scale=-1.0).then_inc(s["decay_done"], 1)

            def take_v(m):
                act.wait_ge(s["v_ready"], m + 1)
                nc.scalar.activation(VB[:, :], PT[:, :], ACT.Copy).then_inc(s["v_copied"], 1)

            def take_r(m):
                act.wait_ge(s["r_ready"], m + 1)
                nc.scalar.activation(RB[0][:, :], PM[:, :], ACT.Copy).then_inc(s["r_copied"], 1)

            def gate_tanh(m):
                act.wait_ge(s["g_ready"], m + 1)
                nc.scalar.activation(GT[:, :], PT[:, :], ACT.Tanh, scale=0.5).then_inc(s["g_tanh"], 1)

            def copy_halves(n, i):
                h = 1 << i
                if i == 0:
                    act.wait_ge(s["r_copied"], n + 1)
                else:
                    act.wait_ge(s["scaled"], n * LEVELS + i)
                    act.wait_ge(s["halves_copied"], n * 2 * LEVELS + 2 * i)
                if 0 <= i - 2 < PAIR_LEVELS:
                    act.wait_ge(s["product_ready"], n * NCH + CH_END[i - 2])
                if i == PAIR_LEVELS + 1:
                    r = halves(RB[PAIR_LEVELS % 4][:, :], 1 << PAIR_LEVELS)[0]
                    nc.scalar.activation(r, ZERO.unsqueeze(2).broadcast_to([P, U >> (PAIR_LEVELS + 1), 1 << PAIR_LEVELS]), ACT.Copy).then_inc(s["left_cleared"], 1)
                if i == 6:
                    act.wait_ge(s["kt_ready"], n * 2 * len(ORDER) + 2)
                nc.scalar.activation(halves(RB[(i + 1) % 4][:, :], h)[0], halves(RB[i % 4][:, :], h)[0], ACT.Copy).then_inc(s["halves_copied"], 1)
                nc.scalar.activation(halves(KB[(i + 1) % 3][:, :], h)[1], halves(KB[i % 3][:, :], h)[1], ACT.Copy).then_inc(s["halves_copied"], 1)

            def take_vt(n):
                for h in range(2):
                    act.wait_ge(s["vt_ready"], n * 2 + h + 1)
                    nc.scalar.activation(half_rows(VT, h), PT[:, h * BANK:(h + 1) * BANK], ACT.Copy).then_inc(s["vt_copied"], 1)

            def take_kt(n, j):
                scale = LMASK if ORDER[j] == 4 else 1.0
                if j > 0:
                    act.wait_ge(s["kv_ready"], n * NTURN + FIRST_TURN[j])
                for h in range(2):
                    act.wait_ge(s["kt_ready"], n * 2 * len(ORDER) + 2 * j + h + 1)
                    nc.scalar.activation(half_rows(KT, h), PT[:, h * BANK:(h + 1) * BANK], ACT.Copy, scale=scale).then_inc(s["kt_copied"], 1)

            def tile(n, l, tau, ln, t0n):
                m = n + 1
                nxt = ln is not None
                copy_halves(n, 0)
                take_vt(n)
                copy_halves(n, 1)
                if nxt:
                    square_centred(m, "a")
                copy_halves(n, 2)
                if nxt:
                    deviation(m, "a", PM[:, BANK:BANK + BT])
                    weight_a(m, ln)
                copy_halves(n, 3)
                if nxt:
                    hidden_tanh(m)
                copy_halves(n, 4)
                if nxt:
                    decay_hidden_tanh(m)
                copy_halves(n, 5)
                take_kt(n, 0)
                copy_halves(n, 6)
                for j in range(1, len(ORDER)):
                    take_kt(n, j)
                act.wait_ge(s["gcentred"], n + 1)
                nc.scalar.activation(flat(SQ), flat(XM), ACT.Square).then_inc(s["gsquared"], 1)
                if nxt:
                    take_k(m)
                act.wait_ge(s["gvar_ready"], n + 1)
                nc.scalar.activation(GSTD[:, :], GSTD[:, :], ACT.Sqrt, bias=EPS, scale=1.0 / HS).then_inc(s["gstd"], 1)
                if nxt:
                    take_decay(m, ln)
                act.wait_ge(s["gback"], n + 1)
                for g in range(G):
                    last = nc.scalar.activation(flat(XM)[:, g * BT:(g + 1) * BT], PO[:, g * BT:(g + 1) * BT], ACT.Identity,
                                                scale=VEC[:, l, V_GNW, g:g + 1], bias=VEC[:, l, V_GNB, g:g + 1])
                last.then_inc(s["gweighted"], 1)
                if nxt:
                    take_v(m)
                square_centred(n, "c")
                if nxt:
                    take_r(m)
                deviation(n, "c", EX[1][:, 0:BT])
                if nxt:
                    gate_tanh(m)
                ffn = KT[:, :, :].rearrange("p c t -> p (c t)")
                act.wait_ge(s["fk_ready"], n + 1)
                nc.scalar.activation(ffn, PO[:, :], ACT.Relu).then_inc(s["fk_relu"], 1)
                act.wait_ge(s["fk_relu"], n + 1)
                nc.scalar.activation(ffn, ffn, ACT.Square).then_inc(s["fk_squared"], 1)
                act.wait_ge(s["fr_ready"], n + 1)
                nc.scalar.activation(flat(SQ), PM[:, :], ACT.Tanh, scale=0.5).then_inc(s["fr_tanh"], 1)

            act.wait_ge(s["const_loaded"], 32)
            act.wait_ge(s["vec_loaded"], 16)
            square_centred(0, "a")
            deviation(0, "a", PM[:, BANK:BANK + BT])
            weight_a(0, 0)
            hidden_tanh(0)
            decay_hidden_tanh(0)
            take_k(0)
            take_decay(0, 0)
            take_v(0)
            take_r(0)
            gate_tanh(0)
            tiles(act, lambda l: None, tile)

        @block.tensor
        def _(pe):
            def square(out_ps, w, rhs, done, half=None):
                for go in range(G) if half is None else (2 * half, 2 * half + 1):
                    for gi in range(G):
                        last = nc.tensor.matmul(out_ps[:, go * BT:(go + 1) * BT], w[:, gi, go * P:(go + 1) * P],
                                                rhs[:, gi * BT:(gi + 1) * BT], start=(gi == 0), stop=(gi == G - 1))
                if half != 0:
                    last.then_inc(done, 1)

            def channel_mean(out_ps, rhs, done):
                for g in range(G):
                    last = nc.tensor.matmul(out_ps, CHMEAN, rhs(g), start=(g == 0), stop=(g == G - 1))
                last.then_inc(done, 1)

            def mean_a(m, t0):
                channel_mean(PM[:, 0:BT], lambda g: X[:, g, :, bass.ds(t0, T)], s["mean_a"])

            def squared_mean(m, k, out_ps):
                pe.wait_ge(s["squared_" + k], m + 1)
                channel_mean(out_ps, lambda g: flat(SQ)[:, g * BT:(g + 1) * BT], s["var_" + k])

            def hidden(m, l):
                pe.wait_ge(s["low_loaded"], (l + 1) * 5 * 16)
                pe.wait_ge(s["xxx_ready"], m + 1)
                xxx = flat(MX[0])
                for g in range(G):
                    nc.tensor.matmul(PM[:, 0:BT], MAA1[:, g, 0:P], xxx[:, g * BT:(g + 1) * BT], start=(g == 0), stop=(g == G - 1))
                for g in range(G):
                    last = nc.tensor.matmul(PM[0:DM, BT:2 * BT], MAA1[:, g, P:P + DM], xxx[:, g * BT:(g + 1) * BT],
                                            start=(g == 0), stop=(g == G - 1))
                last.then_inc(s["hid_ready"], 1)

            def mix(m, f):
                w2, th = (MAA2[DM * f:DM * f + DM, :], TH1[DM * f:DM * f + DM, :]) if f < 4 else (MAA2B, TH2)
                for h in range(2):
                    if f == F_W:
                        pe.wait_ge(s["hid_tanh"], m + 1)
                    else:
                        pe.wait_ge(s["mix_scaled"], m * 2 * NF + 2 * (f - 1) + h + 1)
                    if f == F_V:
                        pe.wait_ge(s["dhid_tanh"], m + 1)
                    for g in (2 * h, 2 * h + 1):
                        last = nc.tensor.matmul(PM[:, g * BT:(g + 1) * BT], w2[:, g * P:(g + 1) * P], th, start=True, stop=True)
                    last.then_inc(s["mix_ready"], 1)

            def decay_hidden(m):
                pe.wait_ge(s["mixed"], m * NF + F_W + 1)
                pe.wait_ge(s["mix_scaled"], m * 2 * NF + 2 * F_K + 1)
                x = flat(MX[MXBUF[F_W]])
                for g in range(G):
                    last = nc.tensor.matmul(PM[DD:2 * DD, 0:BT], DEC1[:, g, :], x[:, g * BT:(g + 1) * BT], start=(g == 0), stop=(g == G - 1))
                last.then_inc(s["dhid_ready"], 1)

            def project(m, l, f, name, out_ps, done, half=None):
                pe.wait_ge(w_loaded[name], (l + 1) * 16)
                pe.wait_ge(s["mixed"], m * NF + f + 1)
                square(out_ps, W[name], flat(MX[MXBUF[f]]), s[done], half)

            def decay(m):
                pe.wait_ge(s["mixed"], (m + 1) * NF)
                for g in range(G):
                    last = nc.tensor.matmul(PM[:, g * BT:(g + 1) * BT], DEC2[:, g * P:(g + 1) * P], DTH, start=True, stop=True)
                last.then_inc(s["dec_ready"], 1)

            def transposes(src, h, done):
                for c in range(h * (C // 2), (h + 1) * (C // 2)):
                    last = nc.tensor.transpose(PT[:, c * P:(c + 1) * P], src[:, c * T:(c + 1) * T], IDENT)
                last.then_inc(done, 1)

            def sum_pairs(n, lo, hi):
                for c in range(lo, hi):
                    i = CHUNKS[c][0]
                    pe.wait_ge(s["product_ready"], n * NCH + c + 1)
                    if c >= 2:
                        pe.wait_ge(s["pairs_used"], n * NCH + c - 1)
                    if i < 0:
                        for j in range(2):
                            last = nc.tensor.matmul(EX[c % 2][:, j * BT:(j + 1) * BT], HEADU[:, 2 * c + j, :],
                                                    PR[c % NPR][:, j * BT:(j + 1) * BT], start=True, stop=True)
                    else:
                        last = nc.tensor.matmul(EX[c % 2][:, :], HEAD, PR[c % NPR][:, :], start=True, stop=True)
                    last.then_inc(s["pairs_summed"], 1)

            def kv(n, t):
                i, q, h = TURNS[t]
                w = 1 << i
                lo, wide = (0, P) if i == LEVELS else (2 * w * q, max(w, DM))
                if t >= 2:
                    pe.wait_ge(s["kv_masked"], n * NTURN + t - 1)
                for j in range(C // 2):
                    c = h * (C // 2) + j
                    last = nc.tensor.matmul(EX[t % 2][:, j * P:(j + 1) * P], KT[lo:lo + wide, c, :], VT[lo:lo + wide, c, :],
                                            start=True, stop=True)
                last.then_inc(s["kv_ready"], 1)

            def apply(n, t):
                i, q, h = TURNS[t]
                if i == LEVELS:
                    return
                w = 1 << i
                lo, wide = (2 * w * q, 2 * w) if w < DM else (2 * w * q + w, w)
                pe.wait_ge(s["kv_masked"], n * NTURN + t + 1)
                if t == 0:
                    pe.wait_ge(s["left_cleared"], n + 1)
                for j in range(C // 2):
                    c = h * (C // 2) + j
                    last = nc.tensor.matmul(PO[lo:lo + wide, c * P:(c + 1) * P], RB[i % 4][:, c * T + lo:c * T + lo + wide], ST[t % NST][:, j, :],
                                            start=False, stop=False, skip_group_check=True)
                last.then_inc(s["applied"], 1)

            def tile(n, l, tau, ln, t0n):
                m = n + 1
                nxt = ln is not None
                pe.wait_ge(s["g_done"], n + 1)
                for h in range(2):
                    transposes(VB, h, s["vt_ready"])
                pe.wait_ge(s["state_done"], n + l + 1)
                sum_pairs(n, 0, 3)
                if nxt:
                    pe.wait_ge(s["tiles_done"], n + 1)
                    mean_a(m, t0n)
                sum_pairs(n, 3, 5)
                if nxt:
                    squared_mean(m, "a", PM[:, BANK:BANK + BT])
                sum_pairs(n, 5, 9)
                if nxt:
                    hidden(m, ln)
                at = 9
                for f in range(NF):
                    sum_pairs(n, at, MIX_AFTER_SUM[f])
                    at = MIX_AFTER_SUM[f]
                    if nxt:
                        mix(m, f)
                        if f == F_K:
                            sum_pairs(n, at, at + 1)
                            at += 1
                            decay_hidden(m)
                sum_pairs(n, at, NCH)
                for h in range(2):
                    pe.wait_ge(s["scaled"], n * LEVELS + 4)
                    pe.wait_ge(s["halves_copied"], n * 2 * LEVELS + 8)
                    pe.wait_ge(s["vt_copied"], n * 2 + h + 1)
                    transposes(KB[4 % 3], h, s["kt_ready"])
                pe.wait_ge(s["tiles_done"], n + 1)
                pe.wait_ge(s["scaled"], (n + 1) * LEVELS)
                pe.wait_ge(s["halves_copied"], (n + 1) * 2 * LEVELS)
                for c in range(C):
                    last = nc.tensor.matmul(PO[:, c * P:(c + 1) * P], RB[LEVELS % 4][:, c * T:(c + 1) * T], STATE[:, c, :],
                                            start=(c % (C // 2) == 0), stop=False, skip_group_check=True)
                last.then_inc(s["carry_used"], 1)
                pe.wait_ge(s["pairs_used"], (n + 1) * NCH)
                for t in range(NTURN):
                    j = ORDER.index(TURNS[t][0])
                    if t - FIRST_TURN[j] < 2:
                        pe.wait_ge(s["kt_copied"], n * 2 * len(ORDER) + 2 * j + t - FIRST_TURN[j] + 1)
                    kv(n, t)
                    if t == FIRST_TURN[j] + 1 and j + 1 < len(ORDER):
                        for h in range(2):
                            transposes(KB[ORDER[j + 1] % 3], h, s["kt_ready"])
                    if t >= 2:
                        apply(n, t - 2)
                apply(n, NTURN - 2)
                apply(n, NTURN - 1)
                for c in range(C):
                    last = nc.tensor.matmul(PO[:, c * P:(c + 1) * P], OE[:, c * T:(c + 1) * T], IDENT,
                                            start=False, stop=True, skip_group_check=True)
                last.then_inc(s["wkv_summed"], 1)
                if nxt:
                    pe.wait_ge(s["kt_copied"], (n + 1) * 2 * len(ORDER))
                    project(m, ln, F_K, "Wk", PT, "k_ready")
                    decay(m)
                    pe.wait_ge(s["k_copied"], m + 1)
                    project(m, ln, F_V, "Wv", PT, "v_ready", 0)
                pe.wait_ge(s["gnormed"], n + 1)
                for c in range(C):
                    last = nc.tensor.transpose(PO[:, c * T:(c + 1) * T], flat(XM)[:, c * P:(c + 1) * P], IDENT)
                last.then_inc(s["gback"], 1)
                if nxt:
                    project(m, ln, F_V, "Wv", PT, "v_ready", 1)
                pe.wait_ge(s["gated"], n + 1)
                pe.wait_ge(w_loaded["Wo"], (l + 1) * 16)
                square(PO, W["Wo"], flat(XM), s["wo_ready"])
                if nxt:
                    pe.wait_ge(s["decay_done"], m + 1)
                    project(m, ln, F_R, "Wr", PM, "r_ready", 0)
                pe.wait_ge(s["x1_ready"], n + 1)
                channel_mean(EX[0][:, 0:BT], lambda g: X[:, g, :, bass.ds(tau * T, T)], s["mean_c"])
                if nxt:
                    project(m, ln, F_R, "Wr", PM, "r_ready", 1)
                squared_mean(n, "c", EX[1][:, 0:BT])
                if nxt:
                    pe.wait_ge(s["v_copied"], m + 1)
                    project(m, ln, F_G, "Wg", PT, "g_ready")
                pe.wait_ge(s["fk_in"], n + 1)
                pe.wait_ge(w_loaded["Wfk"], (l + 1) * 16)
                square(PO, W["Wfk"], flat(MX[0]), s["fk_ready"])
                pe.wait_ge(s["fr_in"], n + 1)
                if nxt:
                    pe.wait_ge(s["r_copied"], m + 1)
                pe.wait_ge(w_loaded["Wfr"], (l + 1) * 16)
                square(PM, W["Wfr"], flat(MX[1]), s["fr_ready"])
                pe.wait_ge(s["fk_squared"], n + 1)
                pe.wait_ge(w_loaded["Wfv"], (l + 1) * 16)
                square(PO, W["Wfv"], KT[:, :, :].rearrange("p c t -> p (c t)"), s["fv_ready"])

            pe.wait_ge(s["const_loaded"], 32)
            pe.wait_ge(s["x_first"], 16)
            mean_a(0, 0)
            squared_mean(0, "a", PM[:, BANK:BANK + BT])
            hidden(0, 0)
            for f in range(NF):
                mix(0, f)
                if f == F_K:
                    decay_hidden(0)
            project(0, 0, F_K, "Wk", PT, "k_ready")
            decay(0)
            pe.wait_ge(s["k_copied"], 1)
            project(0, 0, F_V, "Wv", PT, "v_ready")
            pe.wait_ge(s["decay_done"], 1)
            project(0, 0, F_R, "Wr", PM, "r_ready")
            pe.wait_ge(s["v_copied"], 1)
            project(0, 0, F_G, "Wg", PT, "g_ready")
            pe.wait_ge(s["x_rest"], 16)
            tiles(pe, lambda l: None, tile)

        @block.vector
        def _(dve):
            base, done = [0], [0]

            def step(ins):
                done[0] += 1
                ins.then_inc(s["vec_order"], 1)

            def settle():
                dve.wait_ge(s["vec_order"], base[0] + done[0])

            def chain(ins):
                step(ins)
                settle()

            def xt(t0):
                return X[:, :, :, bass.ds(t0, T)]

            def centre(m, k, t0, mean_ps):
                dve.wait_ge(s["mean_" + k], m + 1)
                mean = mean_ps.rearrange("p (b t) -> p b t", b=B).unsqueeze(1).broadcast_to([P, G, B, T])
                nc.vector.tensor_tensor(XM[:, :, :, :], xt(t0), mean, ALU.subtract).then_inc(s["centred_" + k], 1)

            def unit_variance(m, k, last):
                dve.wait_ge(s["centred_" + k], m + 1)
                dve.wait_ge(s["squared_" + k], m + 1)
                dve.wait_ge(s["std_" + k], m + 1)
                chain(nc.vector.reciprocal(RSTD[:, :, :], RSTD[:, :, :]))
                last(nc.vector.tensor_tensor(XM[:, :, :, :], XM[:, :, :, :], RSTD[:, :, :].unsqueeze(1).broadcast_to([P, G, B, T]), ALU.mult))

            def difference(history, carry):
                chain(nc.vector.tensor_copy(XA[:, :, :, 0], history))
                step(nc.vector.tensor_copy(carry[:, :, :], XA[:, :, :, T]))
                chain(nc.vector.tensor_tensor(SX[:, :, :, :], XA[:, :, :, 0:T], XA[:, :, :, 1:T + 1], ALU.subtract))

            def toward(dst, l, v, done_sem):
                for g in range(G):
                    last = nc.vector.scalar_tensor_tensor(out=dst[:, g, :, :], in0=SX[:, g, :, :], scalar=VEC[:, l, v, g:g + 1],
                                                          in1=XA[:, g, :, 1:T + 1], op0=ALU.mult, op1=ALU.add)
                    if g < G - 1:
                        step(last)
                last.then_inc(done_sem, 1)

            def unit_variance_a(m):
                unit_variance(m, "a", lambda ins: ins.then_inc(s["normed_a"], 1))

            def difference_a(m, l, first):
                history = CTX0[:, C * HS + C:C * HS + 2 * C].rearrange("p (g b) -> p g b", g=G) if first else CARRYA[:, :, :]
                dve.wait_ge(s["weighted_a"], m + 1)
                difference(history, CARRYA)
                toward(MX[0], l, V_MAAX, s["xxx_ready"])

            def scale_mix(m, l, f):
                mx = MX[MXBUF[f]]
                if f == F_K:
                    dve.wait_ge(s["hid_ready"], m + 1)
                if f == F_G:
                    dve.wait_ge(s["dhid_ready"], m + 1)
                for h in range(2):
                    dve.wait_ge(s["mix_ready"], m * 2 * NF + 2 * f + h + 1)
                    for g in (2 * h, 2 * h + 1):
                        last = nc.vector.scalar_tensor_tensor(out=mx[:, g, :, :], in0=PM[:, g * BT:(g + 1) * BT].rearrange("p (b t) -> p b t", b=B),
                                                              scalar=VEC[:, l, V_MAA0 + f, g:g + 1], in1=SX[:, g, :, :], op0=ALU.add, op1=ALU.mult)
                        if g % 2 == 0:
                            step(last)
                    last.then_inc(s["mix_scaled"], 1)

            def gate(m):
                dve.wait_ge(s["g_tanh"], m + 1)
                nc.vector.scalar_tensor_tensor(out=GT[:, :], in0=GT[:, :], scalar=1.0, in1=PT[:, :], op0=ALU.add, op1=ALU.mult).then_inc(s["g_done"], 1)

            def scale_level(n, i):
                h = 1 << i
                wl, wr = pairs(wt(i))
                nk = U // (2 * h)
                if i == 0:
                    dve.wait_ge(s["decay_done"], n + 1)
                    dve.wait_ge(s["k_copied"], n + 1)
                    dve.wait_ge(s["r_copied"], n + 1)
                else:
                    dve.wait_ge(s["scaled"], n * LEVELS + i)
                    dve.wait_ge(s["halves_copied"], n * 2 * LEVELS + 2 * i)
                if 0 <= i - 2 < PAIR_LEVELS:
                    dve.wait_ge(s["product_ready"], n * NCH + CH_END[i - 2])
                if i == 6:
                    dve.wait_ge(s["kt_ready"], n * 2 * len(ORDER) + 2)
                step(nc.vector.tensor_tensor(halves(RB[(i + 1) % 4][:, :], h)[1], halves(RB[i % 4][:, :], h)[1],
                                             wl.unsqueeze(2).broadcast_to([P, nk, h]), ALU.mult))
                step(nc.vector.tensor_tensor(halves(KB[(i + 1) % 3][:, :], h)[0], halves(KB[i % 3][:, :], h)[0],
                                             wr.unsqueeze(2).broadcast_to([P, nk, h]), ALU.mult))
                nc.vector.tensor_tensor(wt(i + 1), wl, wr, ALU.mult).then_inc(s["scaled"], 1)

            def use_pairs(n, lo, hi):
                for c in range(lo, hi):
                    i, k0, nb = CHUNKS[c]
                    dve.wait_ge(s["pairs_summed"], n * NCH + c + 1)
                    if i < 0:
                        nc.vector.tensor_tensor(OE[:, k0:k0 + nb], EX[c % 2][:, :], VB[:, k0:k0 + nb], ALU.mult).then_inc(s["pairs_used"], 1)
                        dve.wait_ge(s["pairs_used"], n * NCH + c + 1)
                        continue
                    h = 1 << i
                    v = halves(VB[:, :], h)[0][:, k0:k0 + nb, :]
                    part = RD[:, :].rearrange("p (k t) -> p k t", t=h)
                    out = QB if h > 1 else RD
                    nc.vector.tensor_tensor(out[:, :].rearrange("p (k t s) -> p k t s", t=h, s=h),
                                            EX[c % 2][:, :].rearrange("p (k t s) -> p k t s", t=h, s=h),
                                            v.unsqueeze(2).broadcast_to([P, nb, h, h]), ALU.mult).then_inc(s["pairs_used"], 1)
                    dve.wait_ge(s["pairs_used"], n * NCH + c + 1)
                    if h > 1:
                        chain(nc.vector.tensor_reduce(out=part[:, k0:k0 + nb, :], in_=QB[:, :].rearrange("p (k t s) -> p k t s", t=h, s=h), axis=AX.X, op=ALU.add))
                    if c + 1 == CH_END[i]:
                        o = halves(OE[:, :], h)[1]
                        chain(nc.vector.tensor_tensor(o, o, part, ALU.add))

            def start_layer(l):
                done[0] = 0
                st = CTX0[:, 0:C * HS].rearrange("p (c j) -> p c j", c=C).unsqueeze(2).broadcast_to([P, C, P // HS, HS])
                hd = HEAD.rearrange("p (h j) -> p h j", j=HS)
                for c in range(C):
                    step(nc.vector.tensor_tensor(STATE[:, c, :].rearrange("p (h j) -> p h j", j=HS), st[:, c, :, :], hd, ALU.mult))
                step(nc.vector.tensor_copy(CARRYC[:, :, :], CTX0[:, C * HS:C * HS + C].rearrange("p (g b) -> p g b", g=G)))
                for g in range(G):
                    last = nc.vector.tensor_scalar(HEADU[:, g, :], HEAD, VEC[:, l, V_U, g:g + 1], None, ALU.mult)
                    if g < G - 1:
                        step(last)
                last.then_inc(s["state_done"], 1)
                assert done[0] == VEC_LAYER, done

            def tile(n, l, tau, ln, t0n):
                m = n + 1
                nxt = ln is not None
                first = VEC_FIRST + (l + 1) * VEC_LAYER
                base[0], done[0] = first + n * VEC_TILE, 0
                dve.wait_ge(s["state_done"], n + l + 1)
                dve.wait_ge(s["v_copied"], n + 1)
                use_pairs(n, 0, 3)
                if nxt:
                    centre(m, "a", t0n, PM[:, 0:BT])
                scale_level(n, 2)
                use_pairs(n, 3, 5)
                if nxt:
                    unit_variance_a(m)
                scale_level(n, 3)
                use_pairs(n, 5, 7)
                if nxt:
                    difference_a(m, ln, ln != l)
                use_pairs(n, 7, 9)
                scale_level(n, 4)
                at = 9
                for f in range(NF):
                    use_pairs(n, at, MIX_AFTER_USE[f])
                    at = MIX_AFTER_USE[f]
                    if nxt:
                        scale_mix(m, ln, f)
                use_pairs(n, at, NCH)
                scale_level(n, 5)
                scale_level(n, 6)
                hmask = HEAD.unsqueeze(1).broadcast_to([P, C // 2, P])
                for t, (i, q, h) in enumerate(TURNS):
                    dve.wait_ge(s["kv_ready"], n * NTURN + t + 1)
                    if t >= NST:
                        dve.wait_ge(s["applied"], n * NAPPLY + APPLIED[t - NST])
                    nc.vector.tensor_tensor(ST[t % NST][:, :, :], EX[t % 2][:, :].rearrange("p (c j) -> p c j", c=C // 2), hmask, ALU.mult).then_inc(s["kv_masked"], 1)
                    if i == LEVELS:
                        rows = STATE[:, h * (C // 2):(h + 1) * (C // 2), :]
                        dec = wt(LEVELS)[:, h * (C // 2):(h + 1) * (C // 2)].unsqueeze(2).broadcast_to([P, C // 2, P])
                        dve.wait_ge(s["carry_used"], n + 1)
                        dve.wait_ge(s["scaled"], (n + 1) * LEVELS)
                        chain(nc.vector.tensor_tensor(rows, rows, dec, ALU.mult))
                        dve.wait_ge(s["kv_masked"], n * NTURN + t + 1)
                        last = nc.vector.tensor_tensor(rows, rows, ST[t % NST][:, :, :], ALU.add)
                        if h == 0:
                            chain(last)
                        else:
                            last.then_inc(s["state_done"], 1)
                            dve.wait_ge(s["state_done"], n + l + 2)
                dve.wait_ge(s["wkv_summed"], n + 1)
                heads = [P, C * (P // HS), HS]
                wkv = PO[:, :].rearrange("p (h j) -> p h j", j=HS)
                chain(nc.vector.tensor_reduce(out=GMEAN[:, :], in_=wkv, axis=AX.X, op=ALU.add))
                chain(nc.vector.tensor_scalar(GMEAN[:, :], GMEAN[:, :], 1.0 / HS, None, ALU.mult))
                nc.vector.tensor_tensor(flat(XM).rearrange("p (h j) -> p h j", j=HS), wkv, GMEAN[:, :].unsqueeze(2).broadcast_to(heads),
                                        ALU.subtract).then_inc(s["gcentred"], 1)
                dve.wait_ge(s["gsquared"], n + 1)
                nc.vector.tensor_reduce(out=GSTD[:, :], in_=flat(SQ).rearrange("p (h j) -> p h j", j=HS), axis=AX.X, op=ALU.add).then_inc(s["gvar_ready"], 1)
                dve.wait_ge(s["gstd"], n + 1)
                chain(nc.vector.reciprocal(GSTD[:, :], GSTD[:, :]))
                dve.wait_ge(s["gcentred"], n + 1)
                nc.vector.tensor_tensor(flat(XM).rearrange("p (h j) -> p h j", j=HS), flat(XM).rearrange("p (h j) -> p h j", j=HS),
                                        GSTD[:, :].unsqueeze(2).broadcast_to(heads), ALU.mult).then_inc(s["gnormed"], 1)
                dve.wait_ge(s["gweighted"], n + 1)
                nc.vector.scalar_tensor_tensor(out=flat(XM), in0=flat(XM), scalar=0.5, in1=GT[:, :], op0=ALU.mult, op1=ALU.mult).then_inc(s["gated"], 1)
                dve.wait_ge(s["wo_ready"], n + 1)
                xn = xt(tau * T)
                nc.vector.tensor_tensor(xn, xn, PO[:, :].rearrange("p (g b t) -> p g b t", g=G, b=B), ALU.add).then_inc(s["x1_ready"], 1)
                dve.wait_ge(s["x1_ready"], n + 1)
                centre(n, "c", tau * T, EX[0][:, 0:BT])
                if nxt:
                    dve.wait_ge(s["mixed"], (m + 1) * NF)
                unit_variance(n, "c", chain)
                for g in range(G):
                    step(nc.vector.tensor_scalar(XA[:, g, :, 1:T + 1], XM[:, g, :, :], VEC[:, l, V_LN2W, g:g + 1], VEC[:, l, V_LN2B, g:g + 1], ALU.mult, ALU.add))
                settle()
                difference(CARRYC[:, :, :], CARRYC)
                if nxt:
                    dve.wait_ge(s["v_ready"], m + 1)
                toward(MX[0], l, V_FK, s["fk_in"])
                toward(MX[1], l, V_FR, s["fr_in"])
                if nxt:
                    scale_level(m, 0)
                    gate(m)
                    scale_level(m, 1)
                dve.wait_ge(s["fr_tanh"], n + 1)
                dve.wait_ge(s["fv_ready"], n + 1)
                chain(nc.vector.scalar_tensor_tensor(out=flat(SQ), in0=flat(SQ), scalar=1.0, in1=PO[:, :], op0=ALU.add, op1=ALU.mult))
                xn = xn.rearrange("p g b t -> p (g b) t")
                nc.vector.scalar_tensor_tensor(out=xn, in0=flat(SQ).rearrange("p (c t) -> p c t", c=C), scalar=0.5,
                                               in1=xn, op0=ALU.mult, op1=ALU.add).then_inc(s["tiles_done"], 1)
                dve.wait_ge(s["tiles_done"], n + 2)
                assert done[0] == VEC_TILE or not nxt, done

            nc.vector.memset(RD[:, 0:1], 0.0).then_inc(s["tiles_done"], 1)
            dve.wait_ge(s["const_loaded"], 32)
            dve.wait_ge(s["vec_loaded"], 16)
            dve.wait_ge(s["x_first"], 16)
            centre(0, "a", 0, PM[:, 0:BT])
            unit_variance_a(0)
            difference_a(0, 0, True)
            for f in range(NF):
                scale_mix(0, 0, f)
            dve.wait_ge(s["x_rest"], 16)
            scale_level(0, 0)
            gate(0)
            scale_level(0, 1)
            assert done[0] == VEC_FIRST, done

            def start(l):
                base[0] = VEC_FIRST + l * (VEC_LAYER + NT * VEC_TILE)
                start_layer(l)

            tiles(dve, start, tile)


_VECS = [("ln1_w",) * 2, ("ln1_b",) * 2, ("ln2_w",) * 2, ("ln2_b",) * 2, ("maa_x",) * 2,
         (1, "maa_w"), (0, "maa_k"), (2, "maa_v"), (3, "maa_r"), (4, "maa_g"),
         ("time_decay",) * 2, ("u", "faaaa"), ("gn_w",) * 2, ("gn_b",) * 2, ("ffn_maa_k", "fmaa_k"), ("ffn_maa_r", "fmaa_r")]
_SQUARES = [("Wk", "Wk"), ("Wv", "Wv"), ("Wr", "Wr"), ("Wg", "Wg"), ("Wo", "Wo"), ("Wfk", "fWk"), ("Wfr", "fWr"), ("Wfv", "fWv")]


def kernel(**inputs):
    import numpy as np
    import concourse.bacc as bacc
    from concourse.bass_utils import run_bass_kernel_spmd

    a = {k: np.asarray(v) for k, v in inputs.items()}

    def chan(v):
        v = np.moveaxis(v, -1, 0)
        return np.ascontiguousarray(np.moveaxis(v.reshape(G, P, *v.shape[1:]), 0, 1))

    x = chan(a["x"])
    vecs = []
    for l, pre in enumerate(("L0_xattn_", "L1_xattn_")):
        cols = []
        for pair in _VECS:
            if isinstance(pair[0], int):
                cols.append(a["L0_xattn_maa_stack"][0, pair[0]] if l == 0 else a[pre + pair[1]])
            else:
                cols.append(a[pre + pair[l]].reshape(E))
        vecs.append(np.stack([chan(c) for c in cols], axis=1))
    order0 = [1, 0, 2, 3, 4]
    w1 = [a["L0_xattn_maa_w1"].reshape(E, NF, DM)[:, order0].reshape(E, NF * DM), a["L1_xattn_maa_w1"]]
    w2 = [a["L0_xattn_maa_w2"][order0].reshape(NF * DM, E), a["L1_xattn_maa_w2"].reshape(NF * DM, E)]
    maa1 = np.stack([w.reshape(G, P, NF * DM).transpose(1, 0, 2) for w in w1])
    maa2 = np.stack(w2)
    dec1 = np.stack([a[k].reshape(G, P, DD).transpose(1, 0, 2) for k in ("L0_xattn_td_w1", "L1_xattn_decay_w1")])
    dec2 = np.stack([a[k] for k in ("L0_xattn_td_w2", "L1_xattn_decay_w2")])
    squares = np.stack([np.stack([a[pre + pair[l]].T.reshape(G, P, E).transpose(1, 0, 2) for pair in _SQUARES])
                        for l, pre in enumerate(("L0_xattn_", "L1_xattn_"))])
    ctx_rows = a["ctx_2048"][:, 0:2 + HS]
    wkv = ctx_rows[:, 2:].reshape(B, G, P, HS).transpose(2, 1, 0, 3).reshape(P, C * HS)
    shift = [chan(ctx_rows[:, r]).reshape(P, C) for r in (0, 1)]
    st = np.concatenate([wkv] + shift, axis=1)
    head = np.kron(np.eye(P // HS, dtype=np.float32), np.ones((HS, HS), np.float32))
    row = np.arange(P)
    const = np.concatenate([np.eye(P, dtype=np.float32), head, np.full((P, P), 1.0 / E, np.float32),
                            (row % 32 < 16).astype(np.float32)[:, None], np.full((P, 1), LN_EPS, np.float32), np.zeros((P, 1), np.float32)], axis=1)
    arrays = {"x": x, "vec": np.stack(vecs, axis=1), "maa1": maa1, "maa2": maa2, "dec1": dec1, "dec2": dec2,
              "squares": squares, "st": st, "const": const}
    arrays = {k: np.ascontiguousarray(v) for k, v in arrays.items()}
    nc = bacc.Bacc("TRN2", target_bir_lowering=False, num_devices=1)
    args = [nc.dram_tensor(k, v.shape, mybir.dt.from_np(v.dtype), kind="ExternalInput").ap() for k, v in arrays.items()]
    args.append(nc.dram_tensor("y", x.shape, mybir.dt.float32, kind="ExternalOutput").ap())
    build(nc, *args)
    r = run_bass_kernel_spmd(nc, [arrays], core_ids=[0])
    y = r.results[0]["y"]
    return np.ascontiguousarray(y.transpose(2, 3, 1, 0).reshape(B, S, E))
```

```python
import concourse.bass as bass
from concourse import mybir
from contextlib import ExitStack

P = 128
E = 512
G = E // P
B = 2
S = 512
NL = 2
HS = 16
T = 128
NT = S // T
C = G * B
BT = B * T
U = C * T
BANK = 512
DM, DD, NF = 32, 64, 5
LEVELS = 7
PAIR_LEVELS = 4
LN_EPS = 1e-5
(V_LN1W, V_LN1B, V_LN2W, V_LN2B, V_MAAX, V_MAA0, V_TD, V_U, V_GNW, V_GNB, V_FK, V_FR) = \
    (0, 1, 2, 3, 4, 5, 10, 11, 12, 13, 14, 15)
NV = 16
F_W, F_K, F_V, F_R, F_G = range(NF)
MXBUF = {F_W: 3, F_K: 0, F_V: 1, F_R: 2, F_G: 3}
ORDER = [PAIR_LEVELS, LEVELS, 5, 6]
VEC_FIRST, VEC_LAYER, VEC_TILE = 41, 12, 68


def build(nc, x_in, vec_in, maa1_in, maa2_in, dec1_in, dec2_in, sq_in, st_in, const_in, out):
    fp32 = mybir.dt.float32
    ALU = mybir.AluOpType
    ACT = mybir.ActivationFunctionType
    AX = mybir.AxisListType

    ctx = ExitStack()
    with ctx:
        def sb(name, shape):
            return ctx.enter_context(nc.sbuf_tensor(name, shape, fp32))

        def ps(name, cols):
            return ctx.enter_context(nc.psum_tensor(name, [P, cols], fp32))

        def sem(name):
            return ctx.enter_context(nc.semaphore(name))

        X = sb("X", [P, G, B, S])
        SQW = ("Wk", "Wv", "Wr", "Wg", "Wo", "Wfk", "Wfr", "Wfv")
        W = {k: sb(k, [P, G, E]) for k in SQW}
        MAA1 = sb("MAA1", [P, G, NF * DM])
        MAA2 = sb("MAA2", [P, E])
        LOWB = sb("LOWB", [P, E])
        MAA2B, DEC2 = LOWB[0:DM, :], LOWB[DD:2 * DD, :]
        DEC1 = sb("DEC1", [P, G, DD])
        VEC = sb("VEC", [P, NL, NV, G])
        CONST = sb("CONST", [P, 3 * P + 3])
        IDENT, HEAD, CHMEAN = (CONST[:, i * P:(i + 1) * P] for i in range(3))
        LMASK, EPS, ZERO = (CONST[:, 3 * P + i:3 * P + i + 1] for i in range(3))
        HEADU = sb("HEADU", [P, G, P])
        CTX0 = sb("CTX0", [P, C * HS + 2 * C])
        XA = sb("XA", [P, G, B, T + 1])
        CARRYA = sb("CARRYA", [P, G, B])
        CARRYC = sb("CARRYC", [P, G, B])
        SX = sb("SX", [P, G, B, T])
        XM = sb("XM", [P, G, B, T])
        SQ = sb("SQ", [P, G, B, T])
        RSTD = sb("RSTD", [P, B, T])
        TH1 = sb("TH1", [P, BT])
        THB = sb("THB", [P, BT])
        TH2, DTH = THB[0:DM, :], THB[DD:2 * DD, :]
        MX = [sb(f"MX{i}", [P, G, B, T]) for i in range(4)]
        RB = [sb(f"RB{i}", [P, U]) for i in range(4)]
        KB = [sb(f"KB{i}", [P, U]) for i in range(3)]
        WT = sb("WT", [P, 2 * U])
        VB = sb("VB", [P, U])
        GT = sb("GT", [P, U])
        OE = sb("OE", [P, U])
        PR = [sb(f"PR{i}", [P, BANK]) for i in range(3)]
        QB = sb("QB", [P, BANK])
        RD = sb("RD", [P, BANK])
        GMEAN = sb("GMEAN", [P, P // HS * C])
        GSTD = sb("GSTD", [P, P // HS * C])
        VT = sb("VT", [P, C, P])
        KT = sb("KT", [P, C, P])
        NST = 3
        ST = [sb(f"ST{i}", [P, C // 2, P]) for i in range(NST)]
        STATE = sb("STATE", [P, C, P])
        PT = ps("PT", 2 * BANK)
        PM = ps("PM", 2 * BANK)
        PO = ps("PO", 2 * BANK)
        EX = [ps(f"EX{i}", BANK) for i in range(2)]

        WOFF = [2 * U - (2 * U >> i) for i in range(LEVELS + 1)]

        def wt(i):
            return WT[:, WOFF[i]:WOFF[i] + (U >> i)]

        def halves(ap, m):
            v = ap.rearrange("p (k h t) -> p k h t", h=2, t=m)
            return v[:, :, 0, :], v[:, :, 1, :]

        def pairs(ap):
            v = ap.rearrange("p (k h) -> p k h", h=2)
            return v[:, :, 0], v[:, :, 1]

        def flat(t):
            return t[:, :, :, :].rearrange("p g b t -> p (g b t)")

        CHUNKS = [(-1, 0, BANK), (-1, BANK, BANK)]
        for i in range(PAIR_LEVELS):
            m = 1 << i
            nb = BANK // (m * m)
            CHUNKS += [(i, k, nb) for k in range(0, U // (2 * m), nb)]
        NCH = len(CHUNKS)
        BUFFER = [c % 3 if c < 6 else (c - 3) % 5 for c in range(NCH)]
        FORMER = [max((b for b in range(c) if BUFFER[b] == BUFFER[c]), default=None) for c in range(NCH)]
        CH_END = {i: max(n for n, c in enumerate(CHUNKS) if c[0] == i) + 1 for i in range(-1, PAIR_LEVELS)}
        TURNS = []
        for i in ORDER:
            for q in range(1 if i == LEVELS else T // (2 << i)):
                TURNS += [(i, q, h) for h in range(2)]
        NTURN = len(TURNS)
        APPLIED = [sum(u[0] != LEVELS for u in TURNS[:t + 1]) for t in range(NTURN)]
        NAPPLY = APPLIED[-1]
        FIRST_TURN = [[u[0] for u in TURNS].index(i) for i in ORDER]
        AHEAD = 12
        MIX_AFTER_PRODUCT = [12, 15]
        MIX_AFTER_SUM = [10, 12]
        MIX_AFTER_USE = [9, 11]
        MIX_AFTER_TURN = {1: F_V, 5: F_R, 9: F_G}
        DECAY_AFTER_TURN = 3
        KEY_AFTER_TURN = {10: 0, 11: 1, 13: 2}
        NEXT_K_AT = 13
        SCALE4_AT = 12
        EARLY = CH_END[2]
        KT_AFTER_TURN = {1: 1, 5: 2, 9: 3}

        PR += [flat(XM)[:, h * BANK:(h + 1) * BANK] for h in range(2)]
        KTS = [flat(SQ), KT[:, :, :].rearrange("p c t -> p (c t)")]
        FGATE = flat(MX[2])

        def kt_rows(j, c):
            return KTS[j % 2][:, c * P:(c + 1) * P]

        def half_rows(t, h):
            return t[:, h * (C // 2):(h + 1) * (C // 2), :].rearrange("p c t -> p (c t)")

        names = """const_loaded x_first x_rest vec_loaded low_loaded out_stored
            vec_order act_order
            mean_a centred_a squared_a var_a std_a
            mean_c centred_c squared_c var_c std_c
            xxx_ready hid_ready hid_tanh mix_ready mix_scaled mixed
            dhid_ready dhid_tanh k_ready v_ready r_ready g_ready dec_ready
            k_copied v_copied r_copied g_done decay_done
            scaled halves_copied product_ready pairs_summed pairs_used part_ready pairs_joined
            vt_ready vt_copied kt_ready kt_copied kv_ready kv_masked carry_used applied state_done
            wkv_summed gcentred gsquared gvar_ready gstd gnormed gback gweighted gated
            normed_a weighted_a left_cleared
            wo_ready x1_ready fk_in fr_in fk_ready fk_relu fk_squared fr_ready fr_gate fv_ready ffn_gated tiles_done""".split()
        s = {k: sem(k) for k in names}
        w_loaded = {k: sem("loaded_" + k) for k in SQW}
        block = ctx.enter_context(nc.Block())


        def tiles(eng, tile):
            for l in range(NL):
                after = l + 1 if l + 1 < NL else None
                with eng.Fori(0, NT - 2) as tau:
                    tile(l * NT + tau, l, tau, l, l, False, (tau + 2) * T)
                tile(l * NT + NT - 2, l, NT - 2, l, after, True, 0)
                tile(l * NT + NT - 1, l, NT - 1, after, after, False, T)

        @block.sync
        def _(sp):
            def low(l):
                sp.dma_start(MAA1[:, :, :], maa1_in[l]).then_inc(s["low_loaded"], 16)
                sp.dma_start(MAA2[:, :], maa2_in[l, 0:P, :]).then_inc(s["low_loaded"], 16)
                sp.dma_start(MAA2B, maa2_in[l, P:P + DM, :]).then_inc(s["low_loaded"], 16)
                sp.dma_start(DEC1[:, :, :], dec1_in[l]).then_inc(s["low_loaded"], 16)
                sp.dma_start(DEC2, dec2_in[l]).then_inc(s["low_loaded"], 16)

            sp.dma_start(X[:, :, :, 0:T], x_in[:, :, :, 0:T]).then_inc(s["x_first"], 16)
            sp.dma_start(CONST[:, :], const_in).then_inc(s["const_loaded"], 16)
            sp.dma_start(CTX0[:, :], st_in[:, :]).then_inc(s["const_loaded"], 16)
            sp.dma_start(VEC[:, :, :, :], vec_in).then_inc(s["vec_loaded"], 16)
            low(0)
            for j, k in enumerate(SQW):
                sp.dma_start(W[k][:, :, :], sq_in[0, j]).then_inc(w_loaded[k], 16)
                if k == "Wg":
                    sp.dma_start(X[:, :, :, T:S], x_in[:, :, :, T:S]).then_inc(s["x_rest"], 16)
            for l in range(1, NL):
                sp.wait_ge(s["mix_ready"], l * NT * 2 * NF)
                sp.wait_ge(s["dhid_ready"], l * NT)
                sp.wait_ge(s["dec_ready"], l * NT)
                low(l)
                for j, k in enumerate(SQW):
                    sp.wait_ge(s[dict(Wk="k_ready", Wv="v_ready", Wr="r_ready", Wg="g_ready", Wo="wo_ready",
                                      Wfk="fk_ready", Wfr="fr_ready", Wfv="fv_ready")[k]], l * NT)
                    sp.dma_start(W[k][:, :, :], sq_in[l, j]).then_inc(w_loaded[k], 16)
            for tau in range(NT):
                sp.wait_ge(s["tiles_done"], (NL - 1) * NT + tau + 2)
                sp.dma_start(out[:, :, :, tau * T:(tau + 1) * T], X[:, :, :, tau * T:(tau + 1) * T]).then_inc(s["out_stored"], 16)
            sp.wait_ge(s["out_stored"], 16 * NT)

        @block.gpsimd
        def _(pool):
            def add_mix(m, f):
                pool.wait_ge(s["mix_scaled"], m * 2 * NF + 2 * f + 2)
                mx = MX[MXBUF[f]]
                nc.gpsimd.tensor_tensor(mx[:, :, :, :], mx[:, :, :, :], XA[:, :, :, 1:T + 1], ALU.add).then_inc(s["mixed"], 1)

            def first_products(m, nxt, lo, hi):
                pool.wait_ge(s["k_copied"], m + 1)
                pool.wait_ge(s["r_copied"], m + 1)
                products(m, nxt, lo, hi)

            def products(n, nxt, lo, hi):
                for c in range(lo, hi):
                    i, k0, nb = CHUNKS[c]
                    if i >= 1 and c == CH_END[i - 1]:
                        pool.wait_ge(s["scaled"], n * LEVELS + i)
                        pool.wait_ge(s["halves_copied"], n * 2 * LEVELS + 2 * i)
                    if c == 6 and nxt:
                        pool.wait_ge(s["weighted_a"], n + 2)
                    elif c == 6:
                        pool.wait_ge(s["fk_in"], n)
                    if FORMER[c] is not None:
                        pool.wait_ge(s["pairs_summed"], n * NCH + FORMER[c] + 1)
                    o = PR[BUFFER[c]]
                    if i < 0:
                        nc.gpsimd.tensor_tensor(o[:, :], RB[0][:, k0:k0 + nb], KB[0][:, k0:k0 + nb], ALU.mult).then_inc(s["product_ready"], 1)
                    else:
                        h = 1 << i
                        r = halves(RB[i % 4][:, :], h)[1][:, k0:k0 + nb, :]
                        k = halves(KB[i % 3][:, :], h)[0][:, k0:k0 + nb, :]
                        shape = [P, nb, h, h]
                        nc.gpsimd.tensor_tensor(o[:, :].rearrange("p (k t s) -> p k t s", t=h, s=h),
                                                r.unsqueeze(3).broadcast_to(shape), k.unsqueeze(2).broadcast_to(shape),
                                                ALU.mult).then_inc(s["product_ready"], 1)

            def tile(n, l, tau, ln, lp, opens, t0p):
                m, p = n + 1, n + 2
                at = AHEAD
                for f, upto in enumerate(MIX_AFTER_PRODUCT):
                    products(n, ln is not None, at, upto)
                    at = upto
                    if ln is not None:
                        add_mix(m, f)
                products(n, ln is not None, at, NCH)
                pool.wait_ge(s["part_ready"], n + 1)
                o = halves(OE[:, :], 1 << (PAIR_LEVELS - 1))[1]
                nc.gpsimd.tensor_tensor(o, o, RD[:, :].rearrange("p (k t) -> p k t", t=1 << (PAIR_LEVELS - 1)), ALU.add).then_inc(s["pairs_joined"], 1)
                if ln is not None:
                    for f in range(len(MIX_AFTER_PRODUCT), NF):
                        add_mix(m, f)
                if ln is not None:
                    first_products(m, lp is not None, 0, AHEAD)
                pool.wait_ge(s["ffn_gated"], n + 1)
                xn = X[:, :, :, bass.ds(tau * T, T)].rearrange("p g b t -> p (g b) t")
                nc.gpsimd.tensor_tensor(xn, xn, FGATE.rearrange("p (c t) -> p c t", c=C), ALU.add).then_inc(s["tiles_done"], 1)

            for f in range(NF):
                add_mix(0, f)
            first_products(0, True, 0, AHEAD)
            tiles(pool, tile)

        @block.scalar
        def _(act):
            def square_centred(m, k):
                act.wait_ge(s["centred_" + k], m + 1)
                nc.scalar.activation(flat(SQ), flat(XM), ACT.Square).then_inc(s["squared_" + k], 1)

            def deviation(m, k, var):
                act.wait_ge(s["var_" + k], m + 1)
                nc.scalar.activation(RSTD[:, :, :], var.rearrange("p (b t) -> p b t", b=B), ACT.Sqrt, bias=EPS).then_inc(s["std_" + k], 1)

            def weight_a(m, l):
                act.wait_ge(s["normed_a"], m + 1)
                for g in range(G):
                    last = nc.scalar.activation(XA[:, g, :, 1:T + 1], XM[:, g, :, :], ACT.Identity,
                                                scale=VEC[:, l, V_LN1W, g:g + 1], bias=VEC[:, l, V_LN1B, g:g + 1])
                last.then_inc(s["weighted_a"], 1)

            def hidden_tanh(m):
                act.wait_ge(s["hid_ready"], m + 1)
                nc.scalar.activation(TH1[:, :], PM[:, 0:BT], ACT.Tanh)
                nc.scalar.activation(TH2, PM[0:DM, BT:2 * BT], ACT.Tanh).then_inc(s["hid_tanh"], 1)

            def decay_hidden_tanh(m):
                act.wait_ge(s["dhid_ready"], m + 1)
                nc.scalar.activation(DTH, PM[DD:2 * DD, 0:BT], ACT.Tanh).then_inc(s["dhid_tanh"], 1)

            def take_k(m):
                act.wait_ge(s["k_ready"], m + 1)
                nc.scalar.activation(KB[0][:, :], PT[:, :], ACT.Copy).then_inc(s["k_copied"], 1)

            def take_decay(m, l):
                act.wait_ge(s["dec_ready"], m + 1)
                for g in range(G):
                    nc.scalar.activation(WT[:, g * BT:(g + 1) * BT], PM[:, g * BT:(g + 1) * BT], ACT.Exp,
                                         bias=VEC[:, l, V_TD, g:g + 1]).then_inc(s["act_order"], 1)
                act.wait_ge(s["act_order"], (m + 1) * G)
                nc.scalar.activation(wt(0), wt(0), ACT.Exp, scale=-1.0).then_inc(s["decay_done"], 1)

            def take_v(m):
                act.wait_ge(s["v_ready"], m + 1)
                nc.scalar.activation(VB[:, :], PT[:, :], ACT.Copy).then_inc(s["v_copied"], 1)

            def take_r(m):
                act.wait_ge(s["r_ready"], m + 1)
                nc.scalar.activation(RB[0][:, :], PM[:, :], ACT.Copy).then_inc(s["r_copied"], 1)

            def take_gate(m):
                act.wait_ge(s["g_ready"], m + 1)
                nc.scalar.activation(GT[:, :], PT[:, :], ACT.Silu).then_inc(s["g_done"], 1)

            def copy_halves(n, i):
                h = 1 << i
                if i == 0:
                    act.wait_ge(s["r_copied"], n + 1)
                else:
                    act.wait_ge(s["scaled"], n * LEVELS + i)
                    act.wait_ge(s["halves_copied"], n * 2 * LEVELS + 2 * i)
                if 0 <= i - 2 < PAIR_LEVELS:
                    act.wait_ge(s["product_ready"], n * NCH + CH_END[i - 2])
                if i == PAIR_LEVELS + 1:
                    r = halves(RB[PAIR_LEVELS % 4][:, :], 1 << PAIR_LEVELS)[0]
                    nc.scalar.activation(r, ZERO.unsqueeze(2).broadcast_to([P, U >> (PAIR_LEVELS + 1), 1 << PAIR_LEVELS]), ACT.Copy).then_inc(s["left_cleared"], 1)
                if i == 6:
                    act.wait_ge(s["kt_ready"], n * 2 * len(ORDER) + 2)
                nc.scalar.activation(halves(RB[(i + 1) % 4][:, :], h)[0], halves(RB[i % 4][:, :], h)[0], ACT.Copy).then_inc(s["halves_copied"], 1)
                nc.scalar.activation(halves(KB[(i + 1) % 3][:, :], h)[1], halves(KB[i % 3][:, :], h)[1], ACT.Copy).then_inc(s["halves_copied"], 1)

            def take_vt(n):
                for h in range(2):
                    act.wait_ge(s["vt_ready"], n * 2 + h + 1)
                    nc.scalar.activation(half_rows(VT, h), PT[:, h * BANK:(h + 1) * BANK], ACT.Copy).then_inc(s["vt_copied"], 1)

            def take_kt(n, j):
                scale = LMASK if ORDER[j] == 4 else 1.0
                if j > 1:
                    act.wait_ge(s["kv_ready"], n * NTURN + FIRST_TURN[j - 1])
                for h in range(2):
                    act.wait_ge(s["kt_ready"], n * 2 * len(ORDER) + 2 * j + h + 1)
                    nc.scalar.activation(KTS[j % 2][:, h * BANK:(h + 1) * BANK], PT[:, h * BANK:(h + 1) * BANK], ACT.Copy, scale=scale).then_inc(s["kt_copied"], 1)

            def tile(n, l, tau, ln, lp, opens, t0p):
                m, p = n + 1, n + 2
                nxt = ln is not None
                copy_halves(n, 4)
                take_kt(n, 0)
                copy_halves(n, 5)
                copy_halves(n, 6)
                take_kt(n, 1)
                if nxt:
                    decay_hidden_tanh(m)
                for j in range(2, len(ORDER)):
                    take_kt(n, j)
                act.wait_ge(s["gcentred"], n + 1)
                nc.scalar.activation(flat(SQ), flat(XM), ACT.Square).then_inc(s["gsquared"], 1)
                if nxt:
                    take_k(m)
                act.wait_ge(s["gvar_ready"], n + 1)
                nc.scalar.activation(GSTD[:, :], GSTD[:, :], ACT.Sqrt, bias=EPS, scale=1.0 / HS).then_inc(s["gstd"], 1)
                if nxt:
                    take_decay(m, ln)
                act.wait_ge(s["gback"], n + 1)
                for g in range(G):
                    last = nc.scalar.activation(flat(XM)[:, g * BT:(g + 1) * BT], PO[:, g * BT:(g + 1) * BT], ACT.Identity,
                                                scale=VEC[:, l, V_GNW, g:g + 1], bias=VEC[:, l, V_GNB, g:g + 1])
                last.then_inc(s["gweighted"], 1)
                if nxt:
                    take_v(m)
                    take_r(m)
                    copy_halves(m, 0)
                square_centred(n, "c")
                if nxt:
                    copy_halves(m, 1)
                deviation(n, "c", EX[1][:, 0:BT])
                if nxt:
                    take_gate(m)
                if lp is not None:
                    square_centred(p, "a")
                ffn = KTS[1]
                act.wait_ge(s["fk_ready"], n + 1)
                nc.scalar.activation(ffn, PO[:, :], ACT.Relu).then_inc(s["fk_relu"], 1)
                if lp is not None:
                    deviation(p, "a", PM[:, BANK:BANK + BT])
                act.wait_ge(s["fk_relu"], n + 1)
                nc.scalar.activation(ffn, ffn, ACT.Square).then_inc(s["fk_squared"], 1)
                if lp is not None:
                    weight_a(p, lp)
                if nxt:
                    copy_halves(m, 2)
                act.wait_ge(s["fr_ready"], n + 1)
                nc.scalar.activation(FGATE, PM[:, :], ACT.Sigmoid).then_inc(s["fr_gate"], 1)
                if nxt:
                    take_vt(m)
                    copy_halves(m, 3)
                if lp is not None:
                    hidden_tanh(p)

            act.wait_ge(s["const_loaded"], 32)
            act.wait_ge(s["vec_loaded"], 16)
            square_centred(0, "a")
            deviation(0, "a", PM[:, BANK:BANK + BT])
            weight_a(0, 0)
            hidden_tanh(0)
            decay_hidden_tanh(0)
            take_k(0)
            take_decay(0, 0)
            take_v(0)
            take_r(0)
            copy_halves(0, 0)
            take_gate(0)
            square_centred(1, "a")
            copy_halves(0, 1)
            deviation(1, "a", PM[:, BANK:BANK + BT])
            weight_a(1, 0)
            copy_halves(0, 2)
            take_vt(0)
            copy_halves(0, 3)
            hidden_tanh(1)
            tiles(act, tile)

        @block.tensor
        def _(pe):
            HALVES = (range(0, G // 2), range(G // 2, G))

            def square(out_ps, w, rhs, done, groups=range(G)):
                for go in groups:
                    for gi in range(G):
                        last = nc.tensor.matmul(out_ps[:, go * BT:(go + 1) * BT], w[:, gi, go * P:(go + 1) * P],
                                                rhs[:, gi * BT:(gi + 1) * BT], start=(gi == 0), stop=(gi == G - 1))
                if G - 1 in groups:
                    last.then_inc(done, 1)

            def channel_mean(out_ps, rhs, done):
                for g in range(G):
                    last = nc.tensor.matmul(out_ps, CHMEAN, rhs(g), start=(g == 0), stop=(g == G - 1))
                last.then_inc(done, 1)

            def mean_a(m, t0):
                channel_mean(PM[:, 0:BT], lambda g: X[:, g, :, bass.ds(t0, T)], s["mean_a"])

            def squared_mean(m, k, out_ps):
                pe.wait_ge(s["squared_" + k], m + 1)
                channel_mean(out_ps, lambda g: flat(SQ)[:, g * BT:(g + 1) * BT], s["var_" + k])

            def hidden(m, l):
                pe.wait_ge(s["low_loaded"], (l + 1) * 5 * 16)
                pe.wait_ge(s["xxx_ready"], m + 1)
                xxx = flat(MX[0])
                for g in range(G):
                    nc.tensor.matmul(PM[:, 0:BT], MAA1[:, g, 0:P], xxx[:, g * BT:(g + 1) * BT], start=(g == 0), stop=(g == G - 1))
                for g in range(G):
                    last = nc.tensor.matmul(PM[0:DM, BT:2 * BT], MAA1[:, g, P:P + DM], xxx[:, g * BT:(g + 1) * BT],
                                            start=(g == 0), stop=(g == G - 1))
                last.then_inc(s["hid_ready"], 1)

            def mix(m, f):
                w2, th = (MAA2[DM * f:DM * f + DM, :], TH1[DM * f:DM * f + DM, :]) if f < 4 else (MAA2B, TH2)
                for h in range(2):
                    if f == F_W:
                        pe.wait_ge(s["hid_tanh"], m + 1)
                    else:
                        pe.wait_ge(s["mix_scaled"], m * 2 * NF + 2 * (f - 1) + h + 1)
                    if f == F_R:
                        pe.wait_ge(s["dhid_tanh"], m + 1)
                    for g in (2 * h, 2 * h + 1):
                        last = nc.tensor.matmul(PM[:, g * BT:(g + 1) * BT], w2[:, g * P:(g + 1) * P], th, start=True, stop=True)
                    last.then_inc(s["mix_ready"], 1)

            def decay_hidden(m):
                pe.wait_ge(s["mixed"], m * NF + F_W + 1)
                pe.wait_ge(s["mix_scaled"], m * 2 * NF + 2 * F_V + 1)
                x = flat(MX[MXBUF[F_W]])
                for g in range(G):
                    last = nc.tensor.matmul(PM[DD:2 * DD, 0:BT], DEC1[:, g, :], x[:, g * BT:(g + 1) * BT], start=(g == 0), stop=(g == G - 1))
                last.then_inc(s["dhid_ready"], 1)

            def project(m, l, f, name, out_ps, done, groups=range(G)):
                pe.wait_ge(w_loaded[name], (l + 1) * 16)
                pe.wait_ge(s["mixed"], m * NF + f + 1)
                square(out_ps, W[name], flat(MX[MXBUF[f]]), s[done], groups)

            def decay(m):
                pe.wait_ge(s["mixed"], (m + 1) * NF)
                for g in range(G):
                    last = nc.tensor.matmul(PM[:, g * BT:(g + 1) * BT], DEC2[:, g * P:(g + 1) * P], DTH, start=True, stop=True)
                last.then_inc(s["dec_ready"], 1)

            def transposes(src, h, done):
                for c in range(h * (C // 2), (h + 1) * (C // 2)):
                    last = nc.tensor.transpose(PT[:, c * P:(c + 1) * P], src[:, c * T:(c + 1) * T], IDENT)
                last.then_inc(done, 1)

            def turn_v(m):
                pe.wait_ge(s["v_copied"], m + 1)
                pe.wait_ge(s["g_done"], m + 1)
                for h in range(2):
                    transposes(VB, h, s["vt_ready"])

            def sum_pairs(n, lo, hi):
                for c in range(lo, hi):
                    i = CHUNKS[c][0]
                    pe.wait_ge(s["product_ready"], n * NCH + c + 1)
                    if c >= 2:
                        pe.wait_ge(s["pairs_used"], n * NCH + c - 1)
                    if i < 0:
                        for j in range(2):
                            last = nc.tensor.matmul(EX[c % 2][:, j * BT:(j + 1) * BT], HEADU[:, 2 * c + j, :],
                                                    PR[BUFFER[c]][:, j * BT:(j + 1) * BT], start=True, stop=True)
                    else:
                        last = nc.tensor.matmul(EX[c % 2][:, :], HEAD, PR[BUFFER[c]][:, :], start=True, stop=True)
                    last.then_inc(s["pairs_summed"], 1)

            def kv(n, t):
                i, q, h = TURNS[t]
                w = 1 << i
                lo, wide = (0, P) if i == LEVELS else (2 * w * q, max(w, DM))
                if t >= 2:
                    pe.wait_ge(s["kv_masked"], n * NTURN + t - 1)
                for j in range(C // 2):
                    c = h * (C // 2) + j
                    last = nc.tensor.matmul(EX[(NCH + t) % 2][:, j * P:(j + 1) * P], kt_rows(ORDER.index(i), c)[lo:lo + wide, :], VT[lo:lo + wide, c, :],
                                            start=True, stop=True)
                last.then_inc(s["kv_ready"], 1)

            def apply(n, t):
                i, q, h = TURNS[t]
                if i == LEVELS:
                    return
                w = 1 << i
                lo, wide = (2 * w * q, 2 * w) if w < DM else (2 * w * q + w, w)
                pe.wait_ge(s["kv_masked"], n * NTURN + t + 1)
                if t == 0:
                    pe.wait_ge(s["left_cleared"], n + 1)
                for j in range(C // 2):
                    c = h * (C // 2) + j
                    last = nc.tensor.matmul(PO[lo:lo + wide, c * P:(c + 1) * P], RB[i % 4][:, c * T + lo:c * T + lo + wide], ST[t % NST][:, j, :],
                                            start=False, stop=False, skip_group_check=True)
                last.then_inc(s["applied"], 1)

            def tile(n, l, tau, ln, lp, opens, t0p):
                m, p = n + 1, n + 2
                nxt = ln is not None
                at = EARLY
                for f, upto in enumerate(MIX_AFTER_SUM):
                    sum_pairs(n, at, upto)
                    at = upto
                    if nxt:
                        mix(m, f)
                sum_pairs(n, at, NEXT_K_AT)
                for h in range(2):
                    pe.wait_ge(s["scaled"], n * LEVELS + 4)
                    pe.wait_ge(s["halves_copied"], n * 2 * LEVELS + 8)
                    pe.wait_ge(s["vt_copied"], n * 2 + h + 1)
                    transposes(KB[4 % 3], h, s["kt_ready"])
                sum_pairs(n, NEXT_K_AT, NCH)
                pe.wait_ge(s["tiles_done"], n + 1)
                pe.wait_ge(s["scaled"], (n + 1) * LEVELS)
                pe.wait_ge(s["halves_copied"], (n + 1) * 2 * LEVELS)
                for c in range(C):
                    last = nc.tensor.matmul(PO[:, c * P:(c + 1) * P], RB[LEVELS % 4][:, c * T:(c + 1) * T], STATE[:, c, :],
                                            start=(c % (C // 2) == 0), stop=False, skip_group_check=True)
                last.then_inc(s["carry_used"], 1)
                for t in range(NTURN):
                    if t < 2:
                        pe.wait_ge(s["pairs_used"], (n + 1) * NCH - 1 + t)
                    j = ORDER.index(TURNS[t][0])
                    if t - FIRST_TURN[j] < 2:
                        pe.wait_ge(s["kt_copied"], n * 2 * len(ORDER) + 2 * j + t - FIRST_TURN[j] + 1)
                    kv(n, t)
                    if t in KT_AFTER_TURN:
                        jn = KT_AFTER_TURN[t]
                        for h in range(2):
                            pe.wait_ge(s["kt_copied"], n * 2 * len(ORDER) + 2 * jn)
                            transposes(KB[ORDER[jn] % 3], h, s["kt_ready"])
                    if t >= 2:
                        apply(n, t - 2)
                    if nxt and t in MIX_AFTER_TURN:
                        mix(m, MIX_AFTER_TURN[t])
                    if nxt and t == DECAY_AFTER_TURN:
                        decay_hidden(m)
                    if nxt and t in KEY_AFTER_TURN:
                        pe.wait_ge(s["kt_copied"], (n + 1) * 2 * len(ORDER))
                        project(m, ln, F_K, "Wk", PT, "k_ready", (KEY_AFTER_TURN[t],))
                apply(n, NTURN - 2)
                apply(n, NTURN - 1)
                pe.wait_ge(s["pairs_joined"], n + 1)
                for c in range(C):
                    last = nc.tensor.matmul(PO[:, c * P:(c + 1) * P], OE[:, c * T:(c + 1) * T], IDENT,
                                            start=False, stop=True, skip_group_check=True)
                last.then_inc(s["wkv_summed"], 1)
                if nxt:
                    project(m, ln, F_K, "Wk", PT, "k_ready", range(len(KEY_AFTER_TURN), G))
                    decay(m)
                    pe.wait_ge(s["k_copied"], m + 1)
                    project(m, ln, F_V, "Wv", PT, "v_ready")
                pe.wait_ge(s["gnormed"], n + 1)
                for c in range(C):
                    last = nc.tensor.transpose(PO[:, c * T:(c + 1) * T], flat(XM)[:, c * P:(c + 1) * P], IDENT)
                last.then_inc(s["gback"], 1)
                if nxt:
                    pe.wait_ge(s["decay_done"], m + 1)
                    project(m, ln, F_R, "Wr", PM, "r_ready", HALVES[0])
                pe.wait_ge(s["gated"], n + 1)
                pe.wait_ge(w_loaded["Wo"], (l + 1) * 16)
                square(PO, W["Wo"], flat(XM), s["wo_ready"])
                if nxt:
                    project(m, ln, F_R, "Wr", PM, "r_ready", HALVES[1])
                pe.wait_ge(s["x1_ready"], n + 1)
                channel_mean(EX[0][:, 0:BT], lambda g: X[:, g, :, bass.ds(tau * T, T)], s["mean_c"])
                if nxt:
                    pe.wait_ge(s["v_copied"], m + 1)
                    project(m, ln, F_G, "Wg", PT, "g_ready", HALVES[0])
                squared_mean(n, "c", EX[1][:, 0:BT])
                if nxt:
                    project(m, ln, F_G, "Wg", PT, "g_ready", HALVES[1])
                    pe.wait_ge(s["r_copied"], m + 1)
                if lp is not None:
                    mean_a(p, t0p)
                if nxt:
                    pe.wait_ge(s["state_done"], m + ln + 1)
                    pe.wait_ge(s["std_c"], n + 1)
                    sum_pairs(m, 0, 2)
                pe.wait_ge(s["fk_in"], n + 1)
                pe.wait_ge(w_loaded["Wfk"], (l + 1) * 16)
                square(PO, W["Wfk"], flat(MX[0]), s["fk_ready"], HALVES[0])
                if nxt:
                    sum_pairs(m, 2, 4)
                square(PO, W["Wfk"], flat(MX[0]), s["fk_ready"], HALVES[1])
                if lp is not None:
                    squared_mean(p, "a", PM[:, BANK:BANK + BT])
                if nxt:
                    sum_pairs(m, 4, 5)
                pe.wait_ge(s["fr_in"], n + 1)
                pe.wait_ge(w_loaded["Wfr"], (l + 1) * 16)
                square(PM, W["Wfr"], flat(MX[1]), s["fr_ready"], HALVES[0])
                if nxt:
                    sum_pairs(m, 5, 6)
                if lp is not None:
                    pe.wait_ge(s["std_a"], p + 1)
                square(PM, W["Wfr"], flat(MX[1]), s["fr_ready"], HALVES[1])
                if nxt:
                    sum_pairs(m, 6, 7)
                    turn_v(m)
                pe.wait_ge(s["fk_squared"], n + 1)
                pe.wait_ge(w_loaded["Wfv"], (l + 1) * 16)
                square(PO, W["Wfv"], KTS[1], s["fv_ready"], HALVES[0])
                if nxt:
                    sum_pairs(m, 7, 8)
                square(PO, W["Wfv"], KTS[1], s["fv_ready"], HALVES[1])
                if lp is not None:
                    pe.wait_ge(s["fr_gate"], n + 1)
                    hidden(p, lp)
                if nxt:
                    sum_pairs(m, 8, EARLY)

            pe.wait_ge(s["const_loaded"], 32)
            pe.wait_ge(s["x_first"], 16)
            mean_a(0, 0)
            squared_mean(0, "a", PM[:, BANK:BANK + BT])
            hidden(0, 0)
            for f in range(NF):
                mix(0, f)
                if f == F_V:
                    decay_hidden(0)
            project(0, 0, F_K, "Wk", PT, "k_ready")
            decay(0)
            pe.wait_ge(s["k_copied"], 1)
            project(0, 0, F_V, "Wv", PT, "v_ready")
            pe.wait_ge(s["decay_done"], 1)
            project(0, 0, F_R, "Wr", PM, "r_ready")
            pe.wait_ge(s["v_copied"], 1)
            project(0, 0, F_G, "Wg", PT, "g_ready")
            pe.wait_ge(s["x_rest"], 16)
            pe.wait_ge(s["r_copied"], 1)
            mean_a(1, T)
            squared_mean(1, "a", PM[:, BANK:BANK + BT])
            pe.wait_ge(s["std_a"], 2)
            pe.wait_ge(s["state_done"], 1)
            sum_pairs(0, 0, 5)
            turn_v(0)
            hidden(1, 0)
            sum_pairs(0, 5, EARLY)
            tiles(pe, tile)

        @block.vector
        def _(dve):
            base, done, skipped = [0], [0], [0]

            def step(ins):
                done[0] += 1
                ins.then_inc(s["vec_order"], 1)

            def settle():
                dve.wait_ge(s["vec_order"], base[0] + done[0])

            def chain(ins):
                step(ins)
                settle()

            def xt(t0):
                return X[:, :, :, bass.ds(t0, T)]

            def centre(m, k, t0, mean_ps):
                dve.wait_ge(s["mean_" + k], m + 1)
                mean = mean_ps.rearrange("p (b t) -> p b t", b=B).unsqueeze(1).broadcast_to([P, G, B, T])
                nc.vector.tensor_tensor(XM[:, :, :, :], xt(t0), mean, ALU.subtract).then_inc(s["centred_" + k], 1)

            def unit_variance(m, k, last):
                dve.wait_ge(s["centred_" + k], m + 1)
                dve.wait_ge(s["squared_" + k], m + 1)
                dve.wait_ge(s["std_" + k], m + 1)
                chain(nc.vector.reciprocal(RSTD[:, :, :], RSTD[:, :, :]))
                last(nc.vector.tensor_tensor(XM[:, :, :, :], XM[:, :, :, :], RSTD[:, :, :].unsqueeze(1).broadcast_to([P, G, B, T]), ALU.mult))

            def difference(history, carry):
                chain(nc.vector.tensor_copy(XA[:, :, :, 0], history))
                step(nc.vector.tensor_copy(carry[:, :, :], XA[:, :, :, T]))
                chain(nc.vector.tensor_tensor(SX[:, :, :, :], XA[:, :, :, 0:T], XA[:, :, :, 1:T + 1], ALU.subtract))

            def toward(dst, l, v, done_sem):
                for g in range(G):
                    last = nc.vector.scalar_tensor_tensor(out=dst[:, g, :, :], in0=SX[:, g, :, :], scalar=VEC[:, l, v, g:g + 1],
                                                          in1=XA[:, g, :, 1:T + 1], op0=ALU.mult, op1=ALU.add)
                    if g < G - 1:
                        step(last)
                last.then_inc(done_sem, 1)

            def unit_variance_a(m):
                unit_variance(m, "a", lambda ins: ins.then_inc(s["normed_a"], 1))

            def difference_a(m, l, first):
                history = CTX0[:, C * HS + C:C * HS + 2 * C].rearrange("p (g b) -> p g b", g=G) if first else CARRYA[:, :, :]
                dve.wait_ge(s["weighted_a"], m + 1)
                difference(history, CARRYA)
                toward(MX[0], l, V_MAAX, s["xxx_ready"])

            def scale_mix(m, l, f):
                mx = MX[MXBUF[f]]
                if f == F_K:
                    dve.wait_ge(s["hid_ready"], m + 1)
                if f == F_G:
                    dve.wait_ge(s["dhid_ready"], m + 1)
                for h in range(2):
                    dve.wait_ge(s["mix_ready"], m * 2 * NF + 2 * f + h + 1)
                    for g in (2 * h, 2 * h + 1):
                        last = nc.vector.scalar_tensor_tensor(out=mx[:, g, :, :], in0=PM[:, g * BT:(g + 1) * BT].rearrange("p (b t) -> p b t", b=B),
                                                              scalar=VEC[:, l, V_MAA0 + f, g:g + 1], in1=SX[:, g, :, :], op0=ALU.add, op1=ALU.mult)
                        if g % 2 == 0:
                            step(last)
                    last.then_inc(s["mix_scaled"], 1)

            def scale_level(n, i):
                h = 1 << i
                wl, wr = pairs(wt(i))
                nk = U // (2 * h)
                if i == 0:
                    dve.wait_ge(s["decay_done"], n + 1)
                    dve.wait_ge(s["k_copied"], n + 1)
                    dve.wait_ge(s["r_copied"], n + 1)
                else:
                    dve.wait_ge(s["scaled"], n * LEVELS + i)
                    dve.wait_ge(s["halves_copied"], n * 2 * LEVELS + 2 * i)
                if 0 <= i - 2 < PAIR_LEVELS:
                    dve.wait_ge(s["product_ready"], n * NCH + CH_END[i - 2])
                if i == 6:
                    dve.wait_ge(s["kt_ready"], n * 2 * len(ORDER) + 2)
                step(nc.vector.tensor_tensor(halves(RB[(i + 1) % 4][:, :], h)[1], halves(RB[i % 4][:, :], h)[1],
                                             wl.unsqueeze(2).broadcast_to([P, nk, h]), ALU.mult))
                step(nc.vector.tensor_tensor(halves(KB[(i + 1) % 3][:, :], h)[0], halves(KB[i % 3][:, :], h)[0],
                                             wr.unsqueeze(2).broadcast_to([P, nk, h]), ALU.mult))
                nc.vector.tensor_tensor(wt(i + 1), wl, wr, ALU.mult).then_inc(s["scaled"], 1)

            def use_pairs(n, lo, hi):
                for c in range(lo, hi):
                    i, k0, nb = CHUNKS[c]
                    dve.wait_ge(s["pairs_summed"], n * NCH + c + 1)
                    if i < 0:
                        nc.vector.tensor_tensor(OE[:, k0:k0 + nb], EX[c % 2][:, :], VB[:, k0:k0 + nb], ALU.mult).then_inc(s["pairs_used"], 1)
                        dve.wait_ge(s["pairs_used"], n * NCH + c + 1)
                        continue
                    h = 1 << i
                    v = halves(VB[:, :], h)[0][:, k0:k0 + nb, :]
                    part = RD[:, :].rearrange("p (k t) -> p k t", t=h)
                    out = QB if h > 1 else RD
                    nc.vector.tensor_tensor(out[:, :].rearrange("p (k t s) -> p k t s", t=h, s=h),
                                            EX[c % 2][:, :].rearrange("p (k t s) -> p k t s", t=h, s=h),
                                            v.unsqueeze(2).broadcast_to([P, nb, h, h]), ALU.mult).then_inc(s["pairs_used"], 1)
                    dve.wait_ge(s["pairs_used"], n * NCH + c + 1)
                    if c + 1 == NCH:
                        nc.vector.tensor_reduce(out=part[:, k0:k0 + nb, :], in_=QB[:, :].rearrange("p (k t s) -> p k t s", t=h, s=h), axis=AX.X, op=ALU.add).then_inc(s["part_ready"], 1)
                        continue
                    if h > 1:
                        chain(nc.vector.tensor_reduce(out=part[:, k0:k0 + nb, :], in_=QB[:, :].rearrange("p (k t s) -> p k t s", t=h, s=h), axis=AX.X, op=ALU.add))
                    if c + 1 == CH_END[i]:
                        o = halves(OE[:, :], h)[1]
                        chain(nc.vector.tensor_tensor(o, o, part, ALU.add))

            def first_pairs(m, ln, lo, hi):
                dve.wait_ge(s["state_done"], m + ln + 1)
                dve.wait_ge(s["v_copied"], m + 1)
                use_pairs(m, lo, hi)

            def start_layer(l):
                before = done[0]
                st = CTX0[:, 0:C * HS].rearrange("p (c j) -> p c j", c=C).unsqueeze(2).broadcast_to([P, C, P // HS, HS])
                hd = HEAD.rearrange("p (h j) -> p h j", j=HS)
                for c in range(C):
                    step(nc.vector.tensor_tensor(STATE[:, c, :].rearrange("p (h j) -> p h j", j=HS), st[:, c, :, :], hd, ALU.mult))
                for g in range(G):
                    last = nc.vector.tensor_scalar(HEADU[:, g, :], HEAD, VEC[:, l, V_U, g:g + 1], None, ALU.mult)
                    if g < G - 1:
                        step(last)
                last.then_inc(s["state_done"], 1)
                assert done[0] - before == VEC_LAYER - 1, [done[0] - before]

            def start_history():
                step(nc.vector.tensor_copy(CARRYC[:, :, :], CTX0[:, C * HS:C * HS + C].rearrange("p (g b) -> p g b", g=G)))

            def tile(n, l, tau, ln, lp, opens, t0p):
                m, p = n + 1, n + 2
                nxt = ln is not None
                first = VEC_FIRST + (l + 1) * VEC_LAYER - skipped[0]
                base[0], done[0] = first + n * VEC_TILE, 0
                at = EARLY
                for f, upto in enumerate(MIX_AFTER_USE):
                    use_pairs(n, at, upto)
                    at = upto
                    if nxt:
                        scale_mix(m, ln, f)
                use_pairs(n, at, SCALE4_AT)
                scale_level(n, 4)
                use_pairs(n, SCALE4_AT, NCH - 3)
                scale_level(n, 5)
                use_pairs(n, NCH - 3, NCH - 2)
                scale_level(n, 6)
                use_pairs(n, NCH - 2, NCH)
                dve.wait_ge(s["tiles_done"], n + 1)
                hmask = HEAD.unsqueeze(1).broadcast_to([P, C // 2, P])
                for t, (i, q, h) in enumerate(TURNS):
                    dve.wait_ge(s["kv_ready"], n * NTURN + t + 1)
                    if t >= NST:
                        dve.wait_ge(s["applied"], n * NAPPLY + APPLIED[t - NST])
                    nc.vector.tensor_tensor(ST[t % NST][:, :, :], EX[(NCH + t) % 2][:, :].rearrange("p (c j) -> p c j", c=C // 2), hmask, ALU.mult).then_inc(s["kv_masked"], 1)
                    if i == LEVELS:
                        rows = STATE[:, h * (C // 2):(h + 1) * (C // 2), :]
                        dec = wt(LEVELS)[:, h * (C // 2):(h + 1) * (C // 2)].unsqueeze(2).broadcast_to([P, C // 2, P])
                        dve.wait_ge(s["carry_used"], n + 1)
                        dve.wait_ge(s["scaled"], (n + 1) * LEVELS)
                        chain(nc.vector.tensor_tensor(rows, rows, dec, ALU.mult))
                        dve.wait_ge(s["kv_masked"], n * NTURN + t + 1)
                        last = nc.vector.tensor_tensor(rows, rows, ST[t % NST][:, :, :], ALU.add)
                        if h == 0:
                            chain(last)
                        else:
                            last.then_inc(s["state_done"], 1)
                            dve.wait_ge(s["state_done"], n + l + 2)
                    if nxt and t in MIX_AFTER_TURN:
                        scale_mix(m, ln, MIX_AFTER_TURN[t])
                dve.wait_ge(s["wkv_summed"], n + 1)
                heads = [P, C * (P // HS), HS]
                wkv = PO[:, :].rearrange("p (h j) -> p h j", j=HS)
                chain(nc.vector.tensor_reduce(out=GMEAN[:, :], in_=wkv, axis=AX.X, op=ALU.add))
                chain(nc.vector.tensor_scalar(GMEAN[:, :], GMEAN[:, :], 1.0 / HS, None, ALU.mult))
                nc.vector.tensor_tensor(flat(XM).rearrange("p (h j) -> p h j", j=HS), wkv, GMEAN[:, :].unsqueeze(2).broadcast_to(heads),
                                        ALU.subtract).then_inc(s["gcentred"], 1)
                dve.wait_ge(s["gsquared"], n + 1)
                nc.vector.tensor_reduce(out=GSTD[:, :], in_=flat(SQ).rearrange("p (h j) -> p h j", j=HS), axis=AX.X, op=ALU.add).then_inc(s["gvar_ready"], 1)
                dve.wait_ge(s["gstd"], n + 1)
                chain(nc.vector.reciprocal(GSTD[:, :], GSTD[:, :]))
                dve.wait_ge(s["gcentred"], n + 1)
                nc.vector.tensor_tensor(flat(XM).rearrange("p (h j) -> p h j", j=HS), flat(XM).rearrange("p (h j) -> p h j", j=HS),
                                        GSTD[:, :].unsqueeze(2).broadcast_to(heads), ALU.mult).then_inc(s["gnormed"], 1)
                if nxt and ln != l:
                    start_layer(ln)
                dve.wait_ge(s["gweighted"], n + 1)
                nc.vector.tensor_tensor(flat(XM), flat(XM), GT[:, :], ALU.mult).then_inc(s["gated"], 1)
                dve.wait_ge(s["wo_ready"], n + 1)
                xn = xt(tau * T)
                nc.vector.tensor_tensor(xn, xn, PO[:, :].rearrange("p (g b t) -> p g b t", g=G, b=B), ALU.add).then_inc(s["x1_ready"], 1)
                dve.wait_ge(s["x1_ready"], n + 1)
                centre(n, "c", tau * T, EX[0][:, 0:BT])
                if nxt:
                    scale_level(m, 0)
                    scale_level(m, 1)
                if nxt:
                    dve.wait_ge(s["mixed"], (m + 1) * NF)
                unit_variance(n, "c", chain)
                for g in range(G):
                    step(nc.vector.tensor_scalar(XA[:, g, :, 1:T + 1], XM[:, g, :, :], VEC[:, l, V_LN2W, g:g + 1], VEC[:, l, V_LN2B, g:g + 1], ALU.mult, ALU.add))
                settle()
                difference(CARRYC[:, :, :], CARRYC)
                if nxt:
                    dve.wait_ge(s["v_ready"], m + 1)
                toward(MX[0], l, V_FK, s["fk_in"])
                if lp is not None:
                    centre(p, "a", t0p, PM[:, 0:BT])
                if nxt and ln != l:
                    start_history()
                if nxt:
                    first_pairs(m, ln, 0, 1)
                toward(MX[1], l, V_FR, s["fr_in"])
                if nxt:
                    first_pairs(m, ln, 1, 4)
                if lp is not None:
                    unit_variance_a(p)
                if nxt:
                    first_pairs(m, ln, 4, 5)
                if lp is not None:
                    dve.wait_ge(s["fk_ready"], n + 1)
                    difference_a(p, lp, opens)
                if nxt:
                    scale_level(m, 2)
                    first_pairs(m, ln, 5, 7)
                    scale_level(m, 3)
                    first_pairs(m, ln, 7, 8)
                dve.wait_ge(s["fr_gate"], n + 1)
                dve.wait_ge(s["fv_ready"], n + 1)
                nc.vector.tensor_tensor(FGATE, FGATE, PO[:, :], ALU.mult).then_inc(s["ffn_gated"], 1)
                if nxt:
                    first_pairs(m, ln, 8, EARLY)
                if lp is not None:
                    assert done[0] - (VEC_LAYER if ln != l else 0) == VEC_TILE, done
                else:
                    skipped[0] += VEC_TILE - done[0]

            nc.vector.memset(RD[:, 0:1], 0.0).then_inc(s["tiles_done"], 1)
            dve.wait_ge(s["const_loaded"], 32)
            dve.wait_ge(s["vec_loaded"], 16)
            dve.wait_ge(s["x_first"], 16)
            centre(0, "a", 0, PM[:, 0:BT])
            start_layer(0)
            start_history()
            unit_variance_a(0)
            difference_a(0, 0, True)
            for f in range(NF):
                scale_mix(0, 0, f)
            dve.wait_ge(s["x_rest"], 16)
            centre(1, "a", T, PM[:, 0:BT])
            scale_level(0, 0)
            scale_level(0, 1)
            unit_variance_a(1)
            first_pairs(0, 0, 0, 2)
            dve.wait_ge(s["mixed"], NF)
            dve.wait_ge(s["k_ready"], 1)
            difference_a(1, 0, False)
            first_pairs(0, 0, 2, 5)
            scale_level(0, 2)
            first_pairs(0, 0, 5, 7)
            scale_level(0, 3)
            first_pairs(0, 0, 7, EARLY)
            assert done[0] - VEC_LAYER == VEC_FIRST, done
            tiles(dve, tile)


_VECS = [("ln1_w",) * 2, ("ln1_b",) * 2, ("ln2_w",) * 2, ("ln2_b",) * 2, ("maa_x",) * 2,
         (1, "maa_w"), (0, "maa_k"), (2, "maa_v"), (3, "maa_r"), (4, "maa_g"),
         ("time_decay",) * 2, ("u", "faaaa"), ("gn_w",) * 2, ("gn_b",) * 2, ("ffn_maa_k", "fmaa_k"), ("ffn_maa_r", "fmaa_r")]
_SQUARES = [("Wk", "Wk"), ("Wv", "Wv"), ("Wr", "Wr"), ("Wg", "Wg"), ("Wo", "Wo"), ("Wfk", "fWk"), ("Wfr", "fWr"), ("Wfv", "fWv")]


def kernel(**inputs):
    import numpy as np
    import concourse.bacc as bacc
    from concourse.bass_utils import run_bass_kernel_spmd

    a = {k: np.asarray(v) for k, v in inputs.items()}

    def chan(v):
        v = np.moveaxis(v, -1, 0)
        return np.ascontiguousarray(np.moveaxis(v.reshape(G, P, *v.shape[1:]), 0, 1))

    x = chan(a["x"])
    vecs = []
    for l, pre in enumerate(("L0_xattn_", "L1_xattn_")):
        cols = []
        for pair in _VECS:
            if isinstance(pair[0], int):
                cols.append(a["L0_xattn_maa_stack"][0, pair[0]] if l == 0 else a[pre + pair[1]])
            else:
                cols.append(a[pre + pair[l]].reshape(E))
        vecs.append(np.stack([chan(c) for c in cols], axis=1))
    order0 = [1, 0, 2, 3, 4]
    w1 = [a["L0_xattn_maa_w1"].reshape(E, NF, DM)[:, order0].reshape(E, NF * DM), a["L1_xattn_maa_w1"]]
    w2 = [a["L0_xattn_maa_w2"][order0].reshape(NF * DM, E), a["L1_xattn_maa_w2"].reshape(NF * DM, E)]
    maa1 = np.stack([w.reshape(G, P, NF * DM).transpose(1, 0, 2) for w in w1])
    maa2 = np.stack(w2)
    dec1 = np.stack([a[k].reshape(G, P, DD).transpose(1, 0, 2) for k in ("L0_xattn_td_w1", "L1_xattn_decay_w1")])
    dec2 = np.stack([a[k] for k in ("L0_xattn_td_w2", "L1_xattn_decay_w2")])
    squares = np.stack([np.stack([a[pre + pair[l]].T.reshape(G, P, E).transpose(1, 0, 2) for pair in _SQUARES])
                        for l, pre in enumerate(("L0_xattn_", "L1_xattn_"))])
    ctx_rows = a["ctx_2048"][:, 0:2 + HS]
    wkv = ctx_rows[:, 2:].reshape(B, G, P, HS).transpose(2, 1, 0, 3).reshape(P, C * HS)
    shift = [chan(ctx_rows[:, r]).reshape(P, C) for r in (0, 1)]
    st = np.concatenate([wkv] + shift, axis=1)
    head = np.kron(np.eye(P // HS, dtype=np.float32), np.ones((HS, HS), np.float32))
    row = np.arange(P)
    const = np.concatenate([np.eye(P, dtype=np.float32), head, np.full((P, P), 1.0 / E, np.float32),
                            (row % 32 < 16).astype(np.float32)[:, None], np.full((P, 1), LN_EPS, np.float32), np.zeros((P, 1), np.float32)], axis=1)
    arrays = {"x": x, "vec": np.stack(vecs, axis=1), "maa1": maa1, "maa2": maa2, "dec1": dec1, "dec2": dec2,
              "squares": squares, "st": st, "const": const}
    arrays = {k: np.ascontiguousarray(v) for k, v in arrays.items()}
    nc = bacc.Bacc("TRN2", target_bir_lowering=False, num_devices=1)
    args = [nc.dram_tensor(k, v.shape, mybir.dt.from_np(v.dtype), kind="ExternalInput").ap() for k, v in arrays.items()]
    args.append(nc.dram_tensor("y", x.shape, mybir.dt.float32, kind="ExternalOutput").ap())
    build(nc, *args)
    r = run_bass_kernel_spmd(nc, [arrays], core_ids=[0])
    y = r.results[0]["y"]
    return np.ascontiguousarray(y.transpose(2, 3, 1, 0).reshape(B, S, E))
```
